# Optimizing a Trainium2 kernel written in Bass

```python
import numpy as np
import jax
import jax.numpy as jnp

def _softmax(x, axis=-1):
    return jax.nn.softmax(x, axis=axis)

def _gelu(x):
    return jax.nn.gelu(x, approximate=True)

def _silu(x):
    return jax.nn.silu(x)

def _sigmoid(x):
    return jax.nn.sigmoid(x)

def _layernorm(x, axis=-1, eps=1e-05):
    m = jnp.mean(x, axis=axis, keepdims=True)
    v = jnp.var(x, axis=axis, keepdims=True)
    return (x - m) / jnp.sqrt(v + eps)

def _scatter_add(tgt, idx, src, axis=0):
    return tgt.at[idx].add(src)

def _segment_sum(src, seg, n):
    return jax.ops.segment_sum(src, seg, n)
kernel_name = 'mk_gnn_preln_d2_gnn_r8_2e2e8d'

def setup_inputs(seed: int=0):
    np.random.seed(seed)
    _w = jnp.asarray

    def _rec_inputs():
        import jax
        import jax.numpy as jnp
        _gk = jax.random.key(seed)
        x = -0.0009044 + 1 * jax.random.normal(jax.random.fold_in(_gk, 1), (6250, 160), jnp.float32)
        src = jax.random.randint(jax.random.fold_in(_gk, 2), (200000,), 0, 6250, jnp.int32)
        dst = jnp.minimum((6250 * jax.random.uniform(jax.random.fold_in(_gk, 3), (200000,)) ** 2.0).astype(jnp.int32), 49999)
        _o = jnp.argsort(dst, stable=True)
        src = src[_o]
        dst = dst[_o]
        edge_attr_3 = 0.00047201 + 1.00023 * jax.random.normal(jax.random.fold_in(_gk, 12), (200000, 3), jnp.float32)
        edge_attr_4 = 0.0012443 + 1.0001 * jax.random.normal(jax.random.fold_in(_gk, 13), (200000, 4), jnp.float32)
        edge_attr_64 = 0.000279952 + 1.00013 * jax.random.normal(jax.random.fold_in(_gk, 14), (200000, 64), jnp.float32)
        node_vec1 = jax.random.uniform(jax.random.fold_in(_gk, 16), (6250, 1), jnp.float32, 0.0, 1)
        return (x, src, dst, edge_attr_3, edge_attr_4, edge_attr_64, node_vec1)
    x, src, dst, edge_attr_3, edge_attr_4, edge_attr_64, node_vec1 = _rec_inputs()

    def _L0_gnn_setup():
        import jax, jax.numpy as jnp
        import numpy as np
        N_NODES = 1250
        N_EDGES = 40000
        MUL0, MUL1 = (64, 32)
        EDGE_DIM = 64
        W_NUMEL = 224
        DENOM = 32.0
        SQRT3 = 3.0 ** 0.5
        INV_SQRT3 = 1.0 / SQRT3
        INV_SQRT2 = 2.0 ** (-0.5)

        def _forward(node_feature, edge_attr, edge_feature, W_skip0, W_skip1, W_nl0, W_nl1, W_fc1, W_fc2, W_out_s, W_out_v, edge_index):
            N = node_feature.shape[0]
            E = edge_attr.shape[0]
            s = node_feature[:, :MUL0]
            v = node_feature[:, MUL0:].reshape(N, MUL1, 3)
            skip_s = s @ W_skip0
            skip_v = jnp.einsum('nmi,mk->nki', v, W_skip1)
            s = s @ W_nl0
            v = jnp.einsum('nmi,mk->nki', v, W_nl1)
            rhat = edge_attr / jnp.linalg.norm(edge_attr, axis=-1, keepdims=True)
            sh1 = SQRT3 * rhat
            w = jax.nn.relu(edge_feature @ W_fc1) @ W_fc2
            w0, w1, w2, w3, w4 = jnp.split(w, [64, 128, 160, 192], axis=-1)
            src, dst = (edge_index[0], edge_index[1])
            xs = s[dst]
            xv = v[dst]
            out0a = w0 * xs
            out0b = w3 * (jnp.einsum('emi,ei->em', xv, sh1) * INV_SQRT3)
            out1a = (w1 * xs)[:, :, None] * sh1[:, None, :]
            out1b = w2[:, :, None] * xv
            out1c = w4[:, :, None] * (jnp.cross(xv, sh1[:, None, :]) * INV_SQRT2)
            tp = jnp.concatenate([out0a, out0b, out1a.reshape(E, -1), out1b.reshape(E, -1), out1c.reshape(E, -1)], axis=-1)
            agg = jax.ops.segment_sum(tp, src, num_segments=N) / DENOM
            agg_s = agg[:, :96]
            agg_v = agg[:, 96:].reshape(N, 128, 3)
            out_s = agg_s @ W_out_s + skip_s
            out_v = jnp.einsum('nmi,mk->nki', agg_v, W_out_v) + skip_v
            fs = jax.nn.silu(out_s[:, :MUL0])
            gate = jax.nn.sigmoid(out_s[:, MUL0:MUL0 + 32])
            gv = gate[:, :, None] * out_v
            return jnp.concatenate([fs, gv.reshape(N, -1)], axis=-1)
        key = jax.random.key(seed)
        ks = jax.random.split(key, 12)

        def lin(k, fi, fo):
            return jax.random.normal(k, (fi, fo), jnp.float32) / np.float32(np.sqrt(fi))
        return {'node_feature': jax.random.normal(ks[0], (N_NODES, MUL0 + 3 * MUL1), jnp.float32), 'edge_attr': jax.random.normal(ks[1], (N_EDGES, 3), jnp.float32), 'edge_feature': jax.random.normal(ks[2], (N_EDGES, EDGE_DIM), jnp.float32), 'W_skip0': lin(ks[3], MUL0, 96), 'W_skip1': lin(ks[4], MUL1, 32), 'W_nl0': lin(ks[5], MUL0, MUL0), 'W_nl1': lin(ks[6], MUL1, MUL1), 'W_fc1': lin(ks[7], EDGE_DIM, 64), 'W_fc2': lin(ks[8], 64, W_NUMEL), 'W_out_s': lin(ks[9], 96, 96), 'W_out_v': lin(ks[10], 128, 32), 'edge_index': jax.random.randint(ks[11], (2, N_EDGES), 0, N_NODES)}
    _L0_gnn_all = _L0_gnn_setup()
    _L0_gnn_in = {k: v for k, v in _L0_gnn_all.items() if k in ('W_skip0', 'W_skip1', 'W_nl0', 'W_nl1', 'W_fc1', 'W_fc2', 'W_out_s', 'W_out_v')}
    del _L0_gnn_all

    def _L1_gnn_setup():
        import jax, jax.numpy as jnp
        import numpy as np
        N, E = (5000, 80000)
        S_IN, V_IN = (64, 32)
        S_MID, V_MID = (96, 128)
        S_OUT, V_OUT = (96, 32)
        R = 64
        FC_HID = 64
        W_NUMEL = 64 + 64 + 32 + 32 + 32
        NUM_NEIGHBORS = 16.0

        def _inv(d):
            return 1.0 / jnp.sqrt(jnp.float32(d))

        def _forward(node_features, node_attr, edge_attr, edge_scalars, lin1_ws, lin1_wv, fc_w1, fc_w2, sc_ws, sc_wv, lin2_ws, lin2_wv, edge_src, edge_dst):
            n = node_features.shape[0]
            s = node_features[:, :S_IN]
            v = node_features[:, S_IN:].reshape(n, V_IN, 3)
            a = node_attr
            sc_s = s @ sc_ws * a * _inv(S_IN)
            sc_v = jnp.einsum('nci,cd->ndi', v, sc_wv) * a[:, :, None] * _inv(V_IN)
            h_s = s @ lin1_ws * a * _inv(S_IN)
            h_v = jnp.einsum('nci,cd->ndi', v, lin1_wv) * a[:, :, None] * _inv(V_IN)
            hid = jax.nn.silu(edge_scalars @ fc_w1 * _inv(R))
            w = hid @ fc_w2 * _inv(FC_HID)
            w1, w2, w3, w4, w5 = jnp.split(w, [64, 128, 160, 192], axis=-1)
            es = h_s[edge_src]
            ev = h_v[edge_src]
            e0 = edge_attr[:, :1]
            e1 = edge_attr[:, 1:4]
            m_s1 = w1 * es * e0
            m_s2 = w4 * jnp.einsum('eci,ei->ec', ev, e1) * _inv(3)
            m_v1 = (w2 * es)[:, :, None] * e1[:, None, :]
            m_v2 = w3[:, :, None] * ev * e0[:, :, None]
            m_v3 = w5[:, :, None] * jnp.cross(ev, e1[:, None, :]) * _inv(2)
            mid_s = jnp.concatenate([m_s1, m_s2], axis=-1)
            mid_v = jnp.concatenate([m_v1, m_v2, m_v3], axis=1)
            inv_nn = 1.0 / jnp.sqrt(jnp.float32(NUM_NEIGHBORS))
            agg_s = jax.ops.segment_sum(mid_s, edge_dst, num_segments=n) * inv_nn
            agg_v = jax.ops.segment_sum(mid_v, edge_dst, num_segments=n) * inv_nn
            o_s = agg_s @ lin2_ws * a * _inv(S_MID)
            o_v = jnp.einsum('nci,cd->ndi', agg_v, lin2_wv) * a[:, :, None] * _inv(V_MID)
            pre_s = sc_s + o_s
            pre_v = sc_v + o_v
            scalars = jax.nn.silu(pre_s[:, :64])
            gates = jax.nn.sigmoid(pre_s[:, 64:96])
            gated = gates[:, :, None] * pre_v
            return jnp.concatenate([scalars, gated.reshape(n, 3 * V_OUT)], axis=-1)
        key = jax.random.key(seed)
        ks = jax.random.split(key, 13)
        return {'node_features': jax.random.normal(ks[0], (N, S_IN + 3 * V_IN), jnp.float32), 'node_attr': jnp.ones((N, 1), jnp.float32), 'edge_src': jax.random.randint(ks[1], (E,), 0, N), 'edge_dst': jax.random.randint(ks[2], (E,), 0, N), 'edge_attr': jax.random.normal(ks[3], (E, 4), jnp.float32), 'edge_scalars': jax.random.normal(ks[4], (E, R), jnp.float32), 'lin1_ws': jax.random.normal(ks[5], (S_IN, S_IN), jnp.float32), 'lin1_wv': jax.random.normal(ks[6], (V_IN, V_IN), jnp.float32), 'fc_w1': jax.random.normal(ks[7], (R, FC_HID), jnp.float32), 'fc_w2': jax.random.normal(ks[8], (FC_HID, W_NUMEL), jnp.float32), 'sc_ws': jax.random.normal(ks[9], (S_IN, S_OUT), jnp.float32), 'sc_wv': jax.random.normal(ks[10], (V_IN, V_OUT), jnp.float32), 'lin2_ws': jax.random.normal(ks[11], (S_MID, S_OUT), jnp.float32), 'lin2_wv': jax.random.normal(ks[12], (V_MID, V_OUT), jnp.float32)}
    _L1_gnn_all = _L1_gnn_setup()
    _L1_gnn_in = {k: v for k, v in _L1_gnn_all.items() if k in ('lin1_ws', 'lin1_wv', 'fc_w1', 'fc_w2', 'sc_ws', 'sc_wv', 'lin2_ws', 'lin2_wv')}
    del _L1_gnn_all
    return {'x': x, 'src': src, 'dst': dst, 'edge_attr_3': edge_attr_3, 'edge_attr_4': edge_attr_4, 'edge_attr_64': edge_attr_64, 'node_vec1': node_vec1, 'L0_gnn_W_skip0': _L0_gnn_in['W_skip0'], 'L0_gnn_W_skip1': _L0_gnn_in['W_skip1'], 'L0_gnn_W_nl0': _L0_gnn_in['W_nl0'], 'L0_gnn_W_nl1': _L0_gnn_in['W_nl1'], 'L0_gnn_W_fc1': _L0_gnn_in['W_fc1'], 'L0_gnn_W_fc2': _L0_gnn_in['W_fc2'], 'L0_gnn_W_out_s': _L0_gnn_in['W_out_s'], 'L0_gnn_W_out_v': _L0_gnn_in['W_out_v'], 'L1_gnn_lin1_ws': _L1_gnn_in['lin1_ws'], 'L1_gnn_lin1_wv': _L1_gnn_in['lin1_wv'], 'L1_gnn_fc_w1': _L1_gnn_in['fc_w1'], 'L1_gnn_fc_w2': _L1_gnn_in['fc_w2'], 'L1_gnn_sc_ws': _L1_gnn_in['sc_ws'], 'L1_gnn_sc_wv': _L1_gnn_in['sc_wv'], 'L1_gnn_lin2_ws': _L1_gnn_in['lin2_ws'], 'L1_gnn_lin2_wv': _L1_gnn_in['lin2_wv']}

def reference(x, src, dst, edge_attr_3, edge_attr_4, edge_attr_64, node_vec1, L0_gnn_W_skip0, L0_gnn_W_skip1, L0_gnn_W_nl0, L0_gnn_W_nl1, L0_gnn_W_fc1, L0_gnn_W_fc2, L0_gnn_W_out_s, L0_gnn_W_out_v, L1_gnn_lin1_ws, L1_gnn_lin1_wv, L1_gnn_fc_w1, L1_gnn_fc_w2, L1_gnn_sc_ws, L1_gnn_sc_wv, L1_gnn_lin2_ws, L1_gnn_lin2_wv):
    import jax
    import jax.numpy as jnp

    def _L0_gnn_ref(node_feature, edge_attr, edge_feature, W_skip0, W_skip1, W_nl0, W_nl1, W_fc1, W_fc2, W_out_s, W_out_v, edge_index):
        import jax, jax.numpy as jnp
        import numpy as np
        N_NODES = 1250
        N_EDGES = 40000
        MUL0, MUL1 = (64, 32)
        EDGE_DIM = 64
        W_NUMEL = 224
        DENOM = 32.0
        SQRT3 = 3.0 ** 0.5
        INV_SQRT3 = 1.0 / SQRT3
        INV_SQRT2 = 2.0 ** (-0.5)

        def _forward(node_feature, edge_attr, edge_feature, W_skip0, W_skip1, W_nl0, W_nl1, W_fc1, W_fc2, W_out_s, W_out_v, edge_index):
            N = node_feature.shape[0]
            E = edge_attr.shape[0]
            s = node_feature[:, :MUL0]
            v = node_feature[:, MUL0:].reshape(N, MUL1, 3)
            skip_s = s @ W_skip0
            skip_v = jnp.einsum('nmi,mk->nki', v, W_skip1)
            s = s @ W_nl0
            v = jnp.einsum('nmi,mk->nki', v, W_nl1)
            rhat = edge_attr / jnp.linalg.norm(edge_attr, axis=-1, keepdims=True)
            sh1 = SQRT3 * rhat
            w = jax.nn.relu(edge_feature @ W_fc1) @ W_fc2
            w0, w1, w2, w3, w4 = jnp.split(w, [64, 128, 160, 192], axis=-1)
            src, dst = (edge_index[0], edge_index[1])
            xs = s[dst]
            xv = v[dst]
            out0a = w0 * xs
            out0b = w3 * (jnp.einsum('emi,ei->em', xv, sh1) * INV_SQRT3)
            out1a = (w1 * xs)[:, :, None] * sh1[:, None, :]
            out1b = w2[:, :, None] * xv
            out1c = w4[:, :, None] * (jnp.cross(xv, sh1[:, None, :]) * INV_SQRT2)
            tp = jnp.concatenate([out0a, out0b, out1a.reshape(E, -1), out1b.reshape(E, -1), out1c.reshape(E, -1)], axis=-1)
            agg = jax.ops.segment_sum(tp, src, num_segments=N) / DENOM
            agg_s = agg[:, :96]
            agg_v = agg[:, 96:].reshape(N, 128, 3)
            out_s = agg_s @ W_out_s + skip_s
            out_v = jnp.einsum('nmi,mk->nki', agg_v, W_out_v) + skip_v
            fs = jax.nn.silu(out_s[:, :MUL0])
            gate = jax.nn.sigmoid(out_s[:, MUL0:MUL0 + 32])
            gv = gate[:, :, None] * out_v
            return jnp.concatenate([fs, gv.reshape(N, -1)], axis=-1)
        return _forward(node_feature, edge_attr, edge_feature, W_skip0, W_skip1, W_nl0, W_nl1, W_fc1, W_fc2, W_out_s, W_out_v, edge_index)

    def _L1_gnn_ref(node_features, node_attr, edge_src, edge_dst, edge_attr, edge_scalars, lin1_ws, lin1_wv, fc_w1, fc_w2, sc_ws, sc_wv, lin2_ws, lin2_wv):
        import jax, jax.numpy as jnp
        import numpy as np
        N, E = (5000, 80000)
        S_IN, V_IN = (64, 32)
        S_MID, V_MID = (96, 128)
        S_OUT, V_OUT = (96, 32)
        R = 64
        FC_HID = 64
        W_NUMEL = 64 + 64 + 32 + 32 + 32
        NUM_NEIGHBORS = 16.0

        def _inv(d):
            return 1.0 / jnp.sqrt(jnp.float32(d))

        def _forward(node_features, node_attr, edge_attr, edge_scalars, lin1_ws, lin1_wv, fc_w1, fc_w2, sc_ws, sc_wv, lin2_ws, lin2_wv, edge_src, edge_dst):
            n = node_features.shape[0]
            s = node_features[:, :S_IN]
            v = node_features[:, S_IN:].reshape(n, V_IN, 3)
            a = node_attr
            sc_s = s @ sc_ws * a * _inv(S_IN)
            sc_v = jnp.einsum('nci,cd->ndi', v, sc_wv) * a[:, :, None] * _inv(V_IN)
            h_s = s @ lin1_ws * a * _inv(S_IN)
            h_v = jnp.einsum('nci,cd->ndi', v, lin1_wv) * a[:, :, None] * _inv(V_IN)
            hid = jax.nn.silu(edge_scalars @ fc_w1 * _inv(R))
            w = hid @ fc_w2 * _inv(FC_HID)
            w1, w2, w3, w4, w5 = jnp.split(w, [64, 128, 160, 192], axis=-1)
            es = h_s[edge_src]
            ev = h_v[edge_src]
            e0 = edge_attr[:, :1]
            e1 = edge_attr[:, 1:4]
            m_s1 = w1 * es * e0
            m_s2 = w4 * jnp.einsum('eci,ei->ec', ev, e1) * _inv(3)
            m_v1 = (w2 * es)[:, :, None] * e1[:, None, :]
            m_v2 = w3[:, :, None] * ev * e0[:, :, None]
            m_v3 = w5[:, :, None] * jnp.cross(ev, e1[:, None, :]) * _inv(2)
            mid_s = jnp.concatenate([m_s1, m_s2], axis=-1)
            mid_v = jnp.concatenate([m_v1, m_v2, m_v3], axis=1)
            inv_nn = 1.0 / jnp.sqrt(jnp.float32(NUM_NEIGHBORS))
            agg_s = jax.ops.segment_sum(mid_s, edge_dst, num_segments=n) * inv_nn
            agg_v = jax.ops.segment_sum(mid_v, edge_dst, num_segments=n) * inv_nn
            o_s = agg_s @ lin2_ws * a * _inv(S_MID)
            o_v = jnp.einsum('nci,cd->ndi', agg_v, lin2_wv) * a[:, :, None] * _inv(V_MID)
            pre_s = sc_s + o_s
            pre_v = sc_v + o_v
            scalars = jax.nn.silu(pre_s[:, :64])
            gates = jax.nn.sigmoid(pre_s[:, 64:96])
            gated = gates[:, :, None] * pre_v
            return jnp.concatenate([scalars, gated.reshape(n, 3 * V_OUT)], axis=-1)
        return _forward(node_features, node_attr, edge_attr, edge_scalars, lin1_ws, lin1_wv, fc_w1, fc_w2, sc_ws, sc_wv, lin2_ws, lin2_wv, edge_src, edge_dst)
    edge_index = jnp.stack([src, dst])
    h = jnp.maximum(_layernorm(x, axis=-1), 0.0)
    x = x + _L0_gnn_ref(h, edge_attr_3, edge_attr_64, L0_gnn_W_skip0, L0_gnn_W_skip1, L0_gnn_W_nl0, L0_gnn_W_nl1, L0_gnn_W_fc1, L0_gnn_W_fc2, L0_gnn_W_out_s, L0_gnn_W_out_v, edge_index)
    h = jnp.maximum(_layernorm(x, axis=-1), 0.0)
    x = x + _L1_gnn_ref(h, node_vec1, src, dst, edge_attr_4, edge_attr_64, L1_gnn_lin1_ws, L1_gnn_lin1_wv, L1_gnn_fc_w1, L1_gnn_fc_w2, L1_gnn_sc_ws, L1_gnn_sc_wv, L1_gnn_lin2_ws, L1_gnn_lin2_wv)
    return x

_drawn_inputs = setup_inputs


def setup_inputs(seed=0):
    import zlib

    import numpy as np

    out = dict(_drawn_inputs(seed))
    spreads = {}
    factors = {}
    for name, (base, spread) in spreads.items():
        noise = np.random.default_rng([zlib.crc32(name.encode()), seed]).standard_normal(out[name].shape)
        drawn = base * np.exp(spread * noise) if base else spread * noise
        out[name] = jnp.asarray(drawn.astype(out[name].dtype))
    for name, factor in factors.items():
        out[name] = (out[name] * factor).astype(out[name].dtype)
    return out
```

```python
import numpy as np
import concourse.bass as bass
from concourse import mybir
from contextlib import ExitStack

FP32 = mybir.dt.float32
INT32 = mybir.dt.int32
ALU = mybir.AluOpType
ACT = mybir.ActivationFunctionType
AX = mybir.AxisListType

P = 125
NODES = 6250
EDGES = 200000
S_CH, V_CH = 64, 32
CH = S_CH + 3 * V_CH
NT = NODES // P
NB = 5
STEPS = NT // NB
G = 8
GROUPS = EDGES // (P * G)
HID = 64
WCOLS = 224
MSG = 96 + 3 * 128
OUT = 96 + 3 * V_CH
ACCS = 4
ACC_ROWS = NODES + P
MAPS = CH + OUT
BANK = 512
W_SS, W_VV, W_SV, W_DOT, W_CROSS = 0, 64, 96, 160, 192


def bc(ap, axis, n):
    ap = ap.unsqueeze(axis)
    shape = list(ap.shape)
    shape[axis] = n
    return ap.to_broadcast(shape)


def wait(engine, sem, value):
    if not isinstance(value, int) or value > 0:
        engine.wait_ge(sem, value)


def loop(engine, first, end, body):
    body(first)
    with engine.Fori(first + 1, end) as i:
        body(i)


class Phase:
    pass


def allocate(nc, ctx):
    k = Phase()

    def sb(name, shape, dt=FP32):
        return ctx.enter_context(nc.sbuf_tensor(name, shape, dt))

    k.ident = sb("ident", [P, P])
    k.earlier = sb("earlier", [P, P])
    k.trash_i = sb("trash_i", [P, 1], INT32)
    k.trash = sb("trash", [P, 1])
    k.attr_c = sb("attr_c", [P, NT])
    k.maps_a = [sb(f"maps_a{l}", [128, MAPS]) for l in (0, 1)]
    k.maps_b = [sb(f"maps_b{l}", [V_CH, MAPS]) for l in (0, 1)]
    k.fc1 = [sb(f"fc1_{l}", [128, 128]) for l in (0, 1)]
    k.fc2 = [sb(f"fc2_{l}", [128, WCOLS]) for l in (0, 1)]
    k.out_s = [sb(f"out_s{l}", [96, 96]) for l in (0, 1)]
    k.out_v = [sb(f"out_v{l}", [128, V_CH]) for l in (0, 1)]
    k.banks = [ctx.enter_context(nc.psum_tensor(f"bank{n}", [128, BANK], FP32)) for n in range(8)]
    k.table = [nc.dram_tensor(f"table{l}", [NODES, CH], FP32).ap() for l in (0, 1)]
    k.skip = [nc.dram_tensor(f"skip{l}", [P, NT * OUT], FP32).ap() for l in (0, 1)]
    k.x1 = nc.dram_tensor("x1", [P, NT * CH], FP32).ap()
    k.rhat = nc.dram_tensor("rhat", [P, GROUPS * G * 3], FP32).ap()
    k.acc = [[nc.dram_tensor(f"acc{l}_{n}", [ACC_ROWS, OUT], FP32).ap() for n in range(ACCS)]
             for l in (0, 1)]
    return k


def setup_phase(nc, k, w, ea3, attr):
    ctx = ExitStack()
    with ctx:
        def sb(name, shape, dt=FP32):
            return ctx.enter_context(nc.sbuf_tensor(name, shape, dt))

        def sem(name):
            return ctx.enter_context(nc.semaphore(name))

        CHUNKS = 4
        EC = GROUPS * G // CHUNKS
        ZC = ACC_ROWS // P * OUT // 3
        zero = sb("zero", [P, ZC])
        ea = sb("ea", [P, CHUNKS, EC * 3])
        sq = sb("sq", [P, EC * 3])
        ss = sb("ss", [P, EC])
        nrm = sb("nrm", [P, EC])
        inv = sb("inv", [P, EC])

        s_cleared, s_zero, s_weights, s_attr = sem("cleared"), sem("zero_ready"), sem("weights"), sem("attr")
        s_zeroed = [sem(f"zeroed{n}") for n in range(4)]
        s_ea = [sem(f"ea_in{c}") for c in range(CHUNKS)]
        s_sum, s_norm, s_step, s_unit, s_stored = (
            sem("sum_sq"), sem("norm"), sem("dve_step"), sem("unit"), sem("rhat_stored"))
        s_filled, s_mask = sem("filled"), sem("masks")
        block = ctx.enter_context(nc.Block())

        zeroing = [(l, n, m) for l in (0, 1) for n in range(ACCS) for m in range(3)]

        @block.sync
        def _(sp):
            for c in range(CHUNKS):
                sp.dma_start(ea[:, c, :], ea3[:, c * EC * 3:(c + 1) * EC * 3]).then_inc(s_ea[c], 16)
            sp.dma_start(k.attr_c[:, :], attr).then_inc(s_attr, 16)
            sp.wait_ge(s_cleared, 1)
            n = 0
            for l in (0, 1):
                a, b, fc1, fc2 = k.maps_a[l], k.maps_b[l], k.fc1[l], k.fc2[l]
                t0 = CH + 96
                for to, of in (
                    (a[0:64, 0:64], w[l]["lin_s"]), (a[0:64, CH:CH + 96], w[l]["skip_s"]),
                    (a[64:96, 64:96], w[l]["lin_v"]), (a[96:128, 96:128], w[l]["lin_v"]),
                    (b[:, 128:160], w[l]["lin_v"]),
                    (a[64:96, t0:t0 + 32], w[l]["skip_v"]), (a[96:128, t0 + 32:t0 + 64], w[l]["skip_v"]),
                    (b[:, t0 + 64:t0 + 96], w[l]["skip_v"]),
                    (fc1[0:64, 0:64], w[l]["fc1"]), (fc1[64:128, 64:128], w[l]["fc1"]),
                    (k.out_s[l][:, :], w[l]["out_s"]),
                    (k.out_v[l][:, :], w[l]["out_v"]),
                ):
                    sp.dma_start(to, of).then_inc(s_weights, 16)
                    n += 1
                for half in (0, 64):
                    for to, of, size in ((W_SS, 0, 64), (W_SV, 64, 64), (W_VV, 128, 32),
                                         (W_DOT, 160, 32), (W_CROSS, 192, 32)):
                        sp.dma_start(fc2[half:half + 64, to:to + size],
                                     w[l]["fc2"][:, of:of + size]).then_inc(s_weights, 16)
                        n += 1
            for c in range(CHUNKS):
                sp.wait_ge(s_unit, c + 1)
                sp.dma_start(k.rhat[:, c * EC * 3:(c + 1) * EC * 3], ea[:, c, :]).then_inc(s_stored, 16)
            sp.wait_ge(s_stored, 16 * CHUNKS)
            sp.wait_ge(s_weights, 16 * n)
            sp.wait_ge(s_attr, 16)

        n_weights = 2 * (12 + 10)

        @block.gpsimd
        def _(pool):
            pool.iota(k.trash_i[:, :], pattern=[[0, 1]], base=NODES, channel_multiplier=1).then_inc(s_mask, 1)
            pool.memset(k.ident[:, :], 0.0).then_inc(s_filled, 1)
            pool.memset(k.earlier[:, :], 1.0).then_inc(s_filled, 1)
            pool.wait_ge(s_filled, 2)
            pool.affine_select(out=k.ident[:, :], in_=k.ident[:, :], compare_op=ALU.not_equal, fill=1.0,
                               base=0, pattern=[[-1, P]], channel_multiplier=1).then_inc(s_mask, 1)
            pool.affine_select(out=k.earlier[:, :], in_=k.earlier[:, :], compare_op=ALU.is_gt, fill=0.0,
                               base=0, pattern=[[-1, P]], channel_multiplier=1).then_inc(s_mask, 1)
            pool.wait_ge(s_mask, 3)

        @block.scalar
        def _(act):
            act.wait_ge(s_zero, 1)
            for n, (l, a, m) in enumerate(zeroing):
                if n >= 4:
                    act.wait_ge(s_zeroed[n % 4], 16 * (n // 4))
                view = k.acc[l][a].rearrange("(p t) c -> p (t c)", p=P)
                act.dma_start(view[:, m * ZC:(m + 1) * ZC], zero[:, :]).then_inc(s_zeroed[n % 4], 16)
            for c in range(CHUNKS):
                act.wait_ge(s_sum, c + 1)
                if c:
                    act.wait_ge(s_unit, c)
                nc.scalar.activation(nrm[:, :], ss[:, :], ACT.Sqrt).then_inc(s_norm, 1)
            for n in range(4):
                act.wait_ge(s_zeroed[n], 16 * len(zeroing) // 4)

        @block.vector
        def _(dve):
            nc.vector.memset(zero[:, :], 0.0).then_inc(s_zero, 1)
            for l in (0, 1):
                for weights in (k.maps_a[l], k.maps_b[l], k.fc1[l]):
                    last = nc.vector.memset(weights[:, :], 0.0)
            last.then_inc(s_cleared, 1)
            steps = 0
            for c in range(CHUNKS):
                v = ea[:, c, :].rearrange("p (e i) -> p e i", i=3)
                dve.wait_ge(s_ea[c], 16)
                nc.vector.tensor_tensor(sq[:, :], ea[:, c, :], ea[:, c, :], ALU.mult).then_inc(s_step, 1)
                dve.wait_ge(s_step, 2 * c + 1)
                nc.vector.tensor_reduce(ss[:, :], sq[:, :].rearrange("p (e i) -> p e i", i=3), AX.X,
                                        ALU.add).then_inc(s_sum, 1)
                dve.wait_ge(s_norm, c + 1)
                nc.vector.reciprocal(inv[:, :], nrm[:, :]).then_inc(s_step, 1)
                dve.wait_ge(s_step, 2 * c + 2)
                nc.vector.tensor_tensor(v, v, bc(inv[:, :], 2, 3), ALU.mult).then_inc(s_unit, 1)
            dve.wait_ge(s_mask, 3)
            nc.vector.tensor_copy(k.trash[:, :], k.trash_i[:, :])
            dve.wait_ge(s_weights, 16 * n_weights)
            r2, r3 = 2.0 ** -0.5, 3.0 ** -0.5
            common1 = (1.0 / HID ** 0.5) * 16.0 ** -0.5
            cs, cv = common1 * 96.0 ** -0.5, common1 * 128.0 ** -0.5
            for weights, lo, hi, factor in (
                (k.out_s[0], 0, 96, 1 / 32.0),
                (k.out_v[0], 0, 64, 3.0 ** 0.5 / 32), (k.out_v[0], 64, 96, 1 / 32.0),
                (k.out_v[0], 96, 128, 3.0 ** 0.5 * r2 / 32),
                (k.maps_a[1], 0, 64, S_CH ** -0.5), (k.maps_a[1], 64, 128, V_CH ** -0.5),
                (k.maps_b[1], 0, 32, V_CH ** -0.5),
                (k.out_s[1], 0, 64, cs), (k.out_s[1], 64, 96, cs * r3),
                (k.out_v[1], 0, 64, cv), (k.out_v[1], 64, 96, cv), (k.out_v[1], 96, 128, cv * r2),
            ):
                part = weights[lo:hi, :]
                nc.vector.tensor_scalar(part, part, factor, None, ALU.mult)


def node_phase(nc, k, phase, x_in, x_out):
    combine, project = phase > 0, phase < 2
    ctx = ExitStack()
    with ctx:
        def sb(name, shape, dt=FP32):
            return ctx.enter_context(nc.sbuf_tensor(f"nodes{phase}_{name}", shape, dt))

        def sem(name):
            return ctx.enter_context(nc.semaphore(f"n{phase}_{name}"))

        x = [sb(f"x{b}", [P, NB, CH]) for b in (0, 1)]
        if combine:
            acc = [sb(f"acc{b}", [P, ACCS, NB, OUT]) for b in (0, 1)]
            skip_in = [sb(f"skip_in{b}", [P, NB, OUT]) for b in (0, 1)]
            gate = sb("gate", [P, NB, 96])
            y = sb("y", [P, NB, CH])
            x1 = sb("sum", [P, NB, CH])
        if project:
            cent = sb("cent", [P, NB, CH])
            square = sb("square", [P, NB, CH])
            sum_x, mean, sum_sq, var, std, rstd = (
                sb(name, [P, NB]) for name in ("sum_x", "mean", "sum_sq", "var", "std", "rstd"))
            h = sb("h", [P, NB, CH])
            hT_a = sb("hT_a", [128, NB, P])
            hT_b = sb("hT_b", [V_CH, NB, P])
            maps = sb("maps", [P, NB, MAPS])
            maps_a, maps_b = k.maps_a[phase], k.maps_b[phase]
        in_dma = [sem(f"in_dma{b}") for b in (0, 1)]
        dve_done, gated, std_ready = sem("dve_done"), sem("gated"), sem("std_ready")
        x1_stored, table_stored, skip_stored = sem("x1_stored"), sem("table_stored"), sem("skip_stored")
        transposed, hT_ready, mapped, maps_ready = (
            sem("transposed"), sem("hT_ready"), sem("mapped"), sem("maps_ready"))
        LOADS = 1 + (ACCS + 1 if combine else 0)
        last = phase - 1

        order = (["pairs", "halves", "pre", "scaled", "scalars", "vectors", "x1"] if combine else []) + (
            ["sum_x", "mean", "cent", "square", "sum_sq", "var", "rstd", "h"] if project else [])
        if phase == 1:
            order.remove("scaled")

        def upto(n, name):
            return n * len(order) + (order.index(name) + 1)

        PRE = "scaled" if phase == 2 else "pre"
        IN_USED = "x1" if combine else "cent"
        block = ctx.enter_context(nc.Block())

        @block.sync
        def _(sp):
            def load(n, b):
                sp.dma_start(x[b][:, :, :].rearrange("p t c -> p (t c)"),
                             x_in[:, bass.ds(n * (NB * CH), NB * CH)]).then_inc(in_dma[b], 16)
                if combine:
                    sp.dma_start(skip_in[b][:, :, :].rearrange("p t c -> p (t c)"),
                                 k.skip[last][:, bass.ds(n * (NB * OUT), NB * OUT)]).then_inc(in_dma[b], 16)
                    for a in range(ACCS):
                        sums = k.acc[last][a][0:NODES, :].rearrange("(p t) c -> p (t c)", p=P)
                        sp.dma_start(acc[b][:, a, :, :].rearrange("p t c -> p (t c)"),
                                     sums[:, bass.ds(n * (NB * OUT), NB * OUT)]).then_inc(in_dma[b], 16)

            load(0, 0)
            load(1, 1)
            with sp.Fori(1, STEPS // 2) as i:
                for b in (0, 1):
                    wait(sp, dve_done, upto(i * 2 + (b - 2), IN_USED))
                    load(i * 2 + b, b)

        @block.vector
        def _(dve):
            def both(i):
                for b in (0, 1):
                    n = i * 2 + b
                    src = x1 if combine else x[b]
                    wait(dve, in_dma[b], (i + 1) * (16 * LOADS))
                    if combine:
                        A, pre, sk = acc[b], acc[b][:, 0, :, :], skip_in[b]
                        nc.vector.tensor_tensor(A[:, 0:2, :, :].rearrange("p a t c -> p (a t c)"),
                                                A[:, 0:2, :, :].rearrange("p a t c -> p (a t c)"),
                                                A[:, 2:4, :, :].rearrange("p a t c -> p (a t c)"),
                                                ALU.add).then_inc(dve_done, 1)
                        wait(dve, dve_done, upto(n, "pairs"))
                        nc.vector.tensor_tensor(pre, pre, A[:, 1, :, :], ALU.add).then_inc(dve_done, 1)
                        wait(dve, dve_done, upto(n, "halves"))
                        nc.vector.tensor_tensor(pre, pre, sk[:, :, :], ALU.add).then_inc(dve_done, 1)
                        wait(dve, dve_done, upto(n, "pre"))
                        if phase == 2:
                            nc.vector.tensor_tensor(
                                pre, pre, bc(k.attr_c[:, bass.ds(n * NB, NB)], 2, OUT),
                                ALU.mult).then_inc(dve_done, 1)
                        wait(dve, gated, n + 1)
                        nc.vector.tensor_tensor(y[:, :, 0:S_CH], pre[:, :, 0:S_CH], gate[:, :, 0:S_CH],
                                                ALU.mult).then_inc(dve_done, 1)
                        for c in range(3):
                            lo = S_CH + V_CH * c
                            ins = nc.vector.tensor_tensor(
                                y[:, :, lo:lo + V_CH], pre[:, :, 96 + V_CH * c:96 + V_CH * (c + 1)],
                                gate[:, :, S_CH:96], ALU.mult)
                        ins.then_inc(dve_done, 1)
                        wait(dve, dve_done, upto(n, "vectors"))
                        wait(dve, x1_stored, n * 16)
                        nc.vector.tensor_tensor(x1[:, :, :], x[b][:, :, :], y[:, :, :],
                                                ALU.add).then_inc(dve_done, 1)
                        wait(dve, dve_done, upto(n, "x1"))
                    if project:
                        nc.vector.tensor_reduce(sum_x[:, :], src[:, :, :], AX.X, ALU.add).then_inc(dve_done, 1)
                        wait(dve, dve_done, upto(n, "sum_x"))
                        nc.vector.tensor_scalar(mean[:, :], sum_x[:, :], 1.0 / CH, None,
                                                ALU.mult).then_inc(dve_done, 1)
                        wait(dve, dve_done, upto(n, "mean"))
                        nc.vector.tensor_tensor(cent[:, :, :], src[:, :, :], bc(mean[:, :], 2, CH),
                                                ALU.subtract).then_inc(dve_done, 1)
                        wait(dve, dve_done, upto(n, "cent"))
                        nc.vector.tensor_tensor(square[:, :, :], cent[:, :, :], cent[:, :, :],
                                                ALU.mult).then_inc(dve_done, 1)
                        wait(dve, dve_done, upto(n, "square"))
                        nc.vector.tensor_reduce(sum_sq[:, :], square[:, :, :], AX.X, ALU.add).then_inc(dve_done, 1)
                        wait(dve, dve_done, upto(n, "sum_sq"))
                        nc.vector.tensor_scalar(var[:, :], sum_sq[:, :], 1.0 / CH, 1e-5, ALU.mult,
                                                ALU.add).then_inc(dve_done, 1)
                        wait(dve, std_ready, n + 1)
                        nc.vector.reciprocal(rstd[:, :], std[:, :]).then_inc(dve_done, 1)
                        wait(dve, dve_done, upto(n, "rstd"))
                        wait(dve, transposed, n)
                        nc.vector.scalar_tensor_tensor(h[:, :, :], cent[:, :, :], 0.0, bc(rstd[:, :], 2, CH),
                                                       ALU.max, ALU.mult).then_inc(dve_done, 1)

            loop(dve, 0, STEPS // 2, both)

        @block.scalar
        def _(act):
            def both(i):
                for b in (0, 1):
                    n = i * 2 + b
                    if combine:
                        wait(act, dve_done, upto(n, PRE))
                        nc.scalar.activation(gate[:, :, :], acc[b][:, 0, :, 0:96], ACT.Sigmoid).then_inc(gated, 1)
                        wait(act, dve_done, upto(n, "x1"))
                        act.dma_start(x_out[:, bass.ds(n * (NB * CH), NB * CH)],
                                      x1[:, :, :].rearrange("p t c -> p (t c)")).then_inc(x1_stored, 16)
                    if project:
                        wait(act, dve_done, upto(n, "var"))
                        nc.scalar.activation(std[:, :], var[:, :], ACT.Sqrt).then_inc(std_ready, 1)
                        wait(act, transposed, n + 1)
                        for to, of, rows in ((hT_a, 0, 128), (hT_b, 2, V_CH)):
                            nc.scalar.activation(
                                to[:, 0:4, :].rearrange("r t p -> r (t p)"),
                                k.banks[of][0:rows, 0:4 * P], ACT.Copy).then_inc(hT_ready, 1)
                        nc.scalar.activation(hT_a[:, 4, :], k.banks[1][:, 0:P], ACT.Copy).then_inc(hT_ready, 1)
                        nc.scalar.activation(hT_b[:, 4, :], k.banks[1][0:V_CH, P:2 * P],
                                             ACT.Copy).then_inc(hT_ready, 1)
                        wait(act, table_stored, n * 16)
                        wait(act, skip_stored, n * 16)
                        for t in range(NB):
                            wait(act, mapped, n * NB + (t + 1))
                            bank = k.banks[3 + t]
                            if phase == 1:
                                nc.scalar.activation(maps[:, t, 0:CH], bank[0:P, 0:CH], ACT.Copy,
                                                     scale=k.attr_c[:, bass.ds(n * NB + t, 1)])
                                nc.scalar.activation(maps[:, t, CH:MAPS], bank[0:P, CH:MAPS],
                                                     ACT.Copy).then_inc(maps_ready, 1)
                            else:
                                nc.scalar.activation(maps[:, t, :], bank[0:P, 0:MAPS],
                                                     ACT.Copy).then_inc(maps_ready, 1)
                        wait(act, maps_ready, (n + 1) * NB)
                        rows = k.table[phase].rearrange("(p t) c -> p t c", p=P)
                        act.dma_start(rows[:, bass.ds(n * NB, NB), :], maps[:, :, 0:CH]).then_inc(table_stored, 16)
                        rows = k.skip[phase].rearrange("p (t c) -> p t c", c=OUT)
                        act.dma_start(rows[:, bass.ds(n * NB, NB), :], maps[:, :, CH:MAPS]).then_inc(skip_stored, 16)
            loop(act, 0, STEPS // 2, both)
            if combine:
                wait(act, x1_stored, STEPS * 16)
            if project:
                wait(act, table_stored, STEPS * 16)
                wait(act, skip_stored, STEPS * 16)

        if project:
            @block.tensor
            def _(pe):
                def step(n):
                    wait(pe, dve_done, upto(n, "h"))
                    wait(pe, hT_ready, n * 4)
                    for t in range(NB):
                        bank, col = (0, t * P) if t < 4 else (1, 0)
                        nc.tensor.transpose(k.banks[bank][:, col:col + P], h[:, t, 0:128], k.ident[:, :])
                        bank, col = (2, t * P) if t < 4 else (1, P)
                        ins = nc.tensor.transpose(k.banks[bank][0:V_CH, col:col + P], h[:, t, 128:CH],
                                                  k.ident[:, :])
                    ins.then_inc(transposed, 1)
                    wait(pe, hT_ready, (n + 1) * 4)
                    wait(pe, maps_ready, n * NB)
                    for t in range(NB):
                        out = k.banks[3 + t][0:P, 0:MAPS]
                        nc.tensor.matmul(out, hT_a[:, t, :], maps_a[:, :], start=True, stop=False)
                        nc.tensor.matmul(out, hT_b[:, t, :], maps_b[:, :], start=False,
                                         stop=True).then_inc(mapped, 1)

                loop(pe, 0, STEPS, step)


def edge_phase(nc, k, layer, ef, idx, keycol, keys, attr):
    A = 3 if layer == 0 else 4
    ctx = ExitStack()
    with ctx:
        def sb(name, shape, dt=FP32):
            return ctx.enter_context(nc.sbuf_tensor(f"e{layer}_{name}", shape, dt))

        def two(name, shape, dt=FP32):
            return [sb(f"{name}{b}", shape, dt) for b in (0, 1)]

        def sem(name):
            return ctx.enter_context(nc.semaphore(f"e{layer}_{name}"))

        def sems(name, n=2):
            return [sem(f"{name}{m}") for m in range(n)]

        ef_in = two("ef", [128, 4 * P])
        idx_in = two("idx", [P, G], INT32)
        key_in = two("key", [P, G], INT32)
        keyrow = two("keyrow", [P, G, P], INT32)
        at_in = two("attr", [P, G, A])
        hid = two("hid", [128, 4 * P])
        wts = two("wts", [P, G, WCOLS])
        xg = two("xg", [P, G, CH])
        msg = two("msg", [P, G, MSG])
        same = two("same", [P, G, P])
        slot = two("slot", [P, G], INT32)
        outs = two("outs", [P, G, OUT])
        e5 = sb("e5", [P, G, 5])
        y5 = sb("y5", [P, G, 5, V_CH])
        q = sb("q", [P, G, S_CH])
        d = sb("d", [P, G, 3, V_CH])
        dd = sb("dd", [P, G, V_CH])
        c1 = sb("c1", [P, G, 3, V_CH])
        c2 = sb("c2", [P, G, 3, V_CH])
        masked = sb("masked", [P, G, P])
        count = sb("count", [P, G])
        away = sb("away", [P, G])
        move = sb("move", [P, G])
        aggT = two("aggT", [128, 4, P])
        fc1, fc2 = k.fc1[layer], k.fc2[layer]
        out_s, out_v = k.out_s[layer], k.out_v[layer]

        hid_ps = k.banks[0]
        w_ps, agg_ps, out_ps = k.banks[1:3], k.banks[3:5], k.banks[5:7]

        indexed, features, loaded, gathered = sems("indexed"), sems("features"), sems("loaded"), sems("gathered")
        hid_psum, hid_ready = sems("hid_psum"), sems("hid_ready")
        messages, summed = sems("messages"), sems("summed")
        w_psum, w_ready = sems("w_psum"), sems("w_ready")
        agg_psum, agg_ready = sems("agg_psum"), sems("agg_ready")
        out_psum, out_ready = sems("out_psum"), sems("out_ready")
        added = [sems(f"added{b}_", G) for b in (0, 1)]
        passed = sem("passed")
        level = sem("level")
        LOADS = 16 * 3
        LEVELS = 5
        block = ctx.enter_context(nc.Block())

        def nth(i, b, q):
            return i * 4 + (2 * b + q // 2)

        def nth_tile(i, b, j):
            return i * 8 + (4 * b + j // 2)

        @block.sync
        def _(sp):
            def load_early(i, b):
                g = i * 2 + b
                wait(sp, gathered[b], i * (16 * G))
                sp.dma_start(idx_in[b][:, :], idx[:, bass.ds(g * G, G)]).then_inc(indexed[b], 16)
                wait(sp, hid_psum[b], i)
                sp.dma_start(ef_in[b][:, :], ef[bass.ds(g * 128, 128), :]).then_inc(features[b], 16)

            def load_late(i, b):
                g = i * 2 + b
                wait(sp, messages[b], i)
                sp.dma_start(key_in[b][:, :], keycol[:, bass.ds(g * G, G)]).then_inc(loaded[b], 16)
                sp.dma_start(at_in[b][:, :, :].rearrange("p g a -> p (g a)"),
                             attr[:, bass.ds(g * (G * A), G * A)]).then_inc(loaded[b], 16)
                row = keys[bass.ds(g, 1), :].to_broadcast([P, G * P])
                sp.dma_start(keyrow[b][:, :, :].rearrange("p g e -> p (g e)"), row).then_inc(loaded[b], 16)

            def both(i):
                load_late(i, 0)
                load_early(i, 1)
                load_late(i, 1)
                load_early(i + 1, 0)

            load_early(0, 0)
            loop(sp, 0, GROUPS // 2 - 1, both)
            load_late(GROUPS // 2 - 1, 0)
            load_early(GROUPS // 2 - 1, 1)
            load_late(GROUPS // 2 - 1, 1)


        @block.gpsimd
        def _(pool):
            def gather(i, b, j):
                pool.indirect_dma_start(xg[b][:, j, :], None, k.table[layer],
                                        bass.IndirectOffsetOnAxis(ap=idx_in[b][:, j:j + 1], axis=0)
                                        ).then_inc(gathered[b], 16)

            def before_gathers(i, b):
                wait(pool, indexed[b], (i + 1) * 16)
                wait(pool, messages[b], i)
                pool.sem_inc(passed, 1)

            def scatter(i, b, j):
                if j % 2 == 0:
                    wait(pool, out_ready[(j // 2) % 2], nth(i, b, j // 2) + 1)
                if j >= ACCS:
                    wait(pool, added[b][j - ACCS], (i + 1) * 16)
                elif b:
                    wait(pool, added[0][j + G - ACCS], (i + 1) * 16)
                else:
                    wait(pool, added[1][j + G - ACCS], i * 16)
                pool.sem_inc(passed, 1)
                pool.indirect_dma_start(k.acc[layer][j % ACCS],
                                        bass.IndirectOffsetOnAxis(ap=slot[b][:, j:j + 1], axis=0),
                                        outs[b][:, j, :], None, compute_op=ALU.add).then_inc(added[b][j], 16)

            for b in (0, 1):
                before_gathers(0, b)
                for j in range(G):
                    gather(0, b, j)
            def both(i):
                for b in (0, 1):
                    before_gathers(i, b)
                    for j in range(G):
                        gather(i, b, j)
                        scatter(i - 1, b, j)

            loop(pool, 1, GROUPS // 2, both)
            for b in (0, 1):
                for j in range(G):
                    scatter(GROUPS // 2 - 1, b, j)
            for b in (0, 1):
                for j in range(G):
                    wait(pool, added[b][j], GROUPS // 2 * 16)

        @block.tensor
        def _(pe):
            def fc1_of(i, b):
                wait(pe, features[b], (i + 1) * 16)
                wait(pe, hid_ready[1 - b], i + b)
                nc.tensor.matmul(hid_ps[:, 0:4 * P], fc1[:, :], ef_in[b][:, :], start=True,
                                 stop=True).then_inc(hid_psum[b], 1)

            def weights(i, b, q):
                if q == 0:
                    wait(pe, hid_ready[b], i + 1)
                wait(pe, w_ready[q % 2], nth(i, b, q))
                half = 64 * (q // 2)
                for j in (0, 1):
                    cols = (2 * (q % 2) + j) * P
                    ins = nc.tensor.matmul(w_ps[q % 2][0:P, j * WCOLS:(j + 1) * WCOLS],
                                           hid[b][half:half + 64, cols:cols + P], fc2[half:half + 64, :],
                                           start=True, stop=True)
                ins.then_inc(w_psum[q % 2], 1)

            def agg(i, b, j):
                if j == 0:
                    wait(pe, messages[b], i + 1)
                wait(pe, agg_ready[j % 2], nth_tile(i, b, j))
                for c in range(4):
                    lo = 0 if c == 0 else 96 + 128 * (c - 1)
                    ins = nc.tensor.matmul(agg_ps[j % 2][:, c * P:(c + 1) * P], msg[b][:, j, lo:lo + 128],
                                           same[b][:, j, :], start=True, stop=True)
                ins.then_inc(agg_psum[j % 2], 1)

            def mapped(i, b, j):
                q = j // 2
                wait(pe, agg_ready[j % 2], nth_tile(i, b, j) + 1)
                if j % 2 == 0:
                    wait(pe, out_ready[q % 2], nth(i, b, q))
                col = (j % 2) * OUT
                to = out_ps[q % 2]
                ins = nc.tensor.matmul(to[0:P, col:col + 96], aggT[j % 2][0:96, 0, :], out_s[:, :],
                                       start=True, stop=True)
                if j == G - 1:
                    ins.then_inc(summed[b], 1)
                for c in range(3):
                    lo = col + 96 + V_CH * c
                    ins = nc.tensor.matmul(to[0:P, lo:lo + V_CH], aggT[j % 2][:, 1 + c, :], out_v[:, :],
                                           start=True, stop=True)
                if j % 2:
                    ins.then_inc(out_psum[q % 2], 1)

            for b in (0, 1):
                fc1_of(0, b)
                for q in range(4):
                    weights(0, b, q)
            def both(i):
                for b in (0, 1):
                    fc1_of(i, b)
                    for j in range(G):
                        agg(i - 1, b, j)
                        if j:
                            mapped(i - 1, b, j - 1)
                        if j % 2:
                            weights(i, b, j // 2)
                    mapped(i - 1, b, G - 1)

            loop(pe, 1, GROUPS // 2, both)
            for b in (0, 1):
                for j in range(G):
                    agg(GROUPS // 2 - 1, b, j)
                    if j:
                        mapped(GROUPS // 2 - 1, b, j - 1)
                mapped(GROUPS // 2 - 1, b, G - 1)

        @block.scalar
        def _(act):
            def hidden(i, b):
                wait(act, hid_psum[b], i + 1)
                if layer == 0:
                    nc.scalar.activation(hid[b][:, :], hid_ps[:, 0:4 * P], ACT.Relu).then_inc(hid_ready[b], 1)
                else:
                    nc.scalar.activation(hid[b][:, :], hid_ps[:, 0:4 * P], ACT.Silu,
                                         scale=HID ** -0.5).then_inc(hid_ready[b], 1)

            def weights(i, b, q):
                if q == 0:
                    wait(act, messages[b], i)
                wait(act, w_psum[q % 2], nth(i, b, q) + 1)
                nc.scalar.activation(wts[b][:, 2 * q:2 * q + 2, :].rearrange("p j w -> p (j w)"),
                                     w_ps[q % 2][0:P, 0:2 * WCOLS], ACT.Copy).then_inc(w_ready[q % 2], 1)

            def agg(i, b, j):
                wait(act, agg_psum[j % 2], nth_tile(i, b, j) + 1)
                nc.scalar.activation(aggT[j % 2][:, :, :].rearrange("c m e -> c (m e)"),
                                     agg_ps[j % 2][:, 0:4 * P], ACT.Copy).then_inc(agg_ready[j % 2], 1)

            def pair_out(i, b, q):
                wait(act, out_psum[q % 2], nth(i, b, q) + 1)
                wait(act, added[b][2 * q], i * 16)
                wait(act, added[b][2 * q + 1], i * 16)
                nc.scalar.activation(outs[b][:, 2 * q:2 * q + 2, :].rearrange("p j c -> p (j c)"),
                                     out_ps[q % 2][0:P, 0:2 * OUT], ACT.Copy).then_inc(out_ready[q % 2], 1)

            def sums(i, b, next_weights):
                for j in range(G):
                    agg(i, b, j)
                    if j and j % 2 == 0:
                        pair_out(i, b, j // 2 - 1)
                    if j % 2:
                        next_weights(j // 2)
                pair_out(i, b, G // 2 - 1)

            for b in (0, 1):
                hidden(0, b)
                for q in range(4):
                    weights(0, b, q)
            def both(i):
                for b in (0, 1):
                    hidden(i, b)
                    sums(i - 1, b, lambda q: weights(i, b, q))

            loop(act, 1, GROUPS // 2, both)
            for b in (0, 1):
                sums(GROUPS // 2 - 1, b, lambda q: None)

        @block.vector
        def _(dve):
            def both(i):
                for b in (0, 1):
                    n = i * 2 + b
                    tt = nc.vector.tensor_tensor

                    def reached(l):
                        wait(dve, level, n * LEVELS + l)

                    W, X, M, S = wts[b], xg[b], msg[b], same[b]
                    V = X[:, :, S_CH:CH].rearrange("p g (c m) -> p g c m", c=3)
                    MV = M[:, :, 96:MSG].rearrange("p g (c m) -> p g c m", c=3)
                    keys_c = key_in[b][:, :]
                    e1 = e5[:, :, 0:3]

                    wait(dve, loaded[b], (i + 1) * LOADS)
                    wait(dve, summed[b], i)
                    tt(S[:, :, :], keyrow[b][:, :, :], bc(keys_c, 2, P), ALU.is_equal)
                    nc.vector.tensor_copy(e5[:, :, 3:5], at_in[b][:, :, A - 3:A - 1])
                    nc.vector.tensor_copy(e1, at_in[b][:, :, A - 3:A]).then_inc(level, 1)
                    reached(1)
                    for j in range(G):
                        ins = nc.vector.tensor_tensor_reduce(
                            out=masked[:, j, :], in0=S[:, j, :], in1=k.earlier[:, :], scale=1.0, scalar=0.0,
                            op0=ALU.mult, op1=ALU.add, accum_out=count[:, j:j + 1])
                    ins = nc.vector.tensor_scalar(away[:, :], keys_c, -1.0, k.trash[:, 0:1], ALU.mult, ALU.add)
                    if layer == 0:
                        ins.then_inc(level, 1)
                    for bank in (0, 1):
                        wait(dve, w_ready[bank], nth(i, b, 2) + 1)
                    if layer == 1:
                        tt(W[:, :, 0:W_SV], W[:, :, 0:W_SV], bc(at_in[b][:, :, 0], 2, W_SV),
                           ALU.mult).then_inc(level, 1)
                    wait(dve, gathered[b], (i + 1) * (16 * G))
                    reached(2)
                    tt(q[:, :, :], W[:, :, W_SV:W_DOT], X[:, :, 0:S_CH], ALU.mult)
                    tt(d[:, :, :, :], V, bc(e1, 3, V_CH), ALU.mult)
                    tt(y5[:, :, 0:3, :], V, bc(W[:, :, W_CROSS:WCOLS], 2, 3), ALU.mult)
                    tt(y5[:, :, 3:5, :], V[:, :, 0:2, :], bc(W[:, :, W_CROSS:WCOLS], 2, 2), ALU.mult)
                    tt(M[:, :, 0:S_CH], W[:, :, W_SS:W_VV], X[:, :, 0:S_CH], ALU.mult)
                    tt(MV[:, :, :, 64:96], V, bc(W[:, :, W_VV:W_SV], 2, 3), ALU.mult)
                    nc.vector.scalar_tensor_tensor(move[:, :], count[:, :], 1.0, away[:, :],
                                                   ALU.min, ALU.mult).then_inc(level, 1)
                    reached(3)
                    tt(MV[:, :, :, 0:64], bc(q[:, :, :], 2, 3), bc(e1, 3, S_CH), ALU.mult)
                    tt(c1[:, :, :, :], y5[:, :, 1:4, :], bc(e5[:, :, 2:5], 3, V_CH), ALU.mult)
                    tt(c2[:, :, :, :], y5[:, :, 2:5, :], bc(e5[:, :, 1:4], 3, V_CH), ALU.mult)
                    tt(dd[:, :, :], d[:, :, 0, :], d[:, :, 1, :], ALU.add).then_inc(level, 1)
                    reached(4)
                    tt(dd[:, :, :], dd[:, :, :], d[:, :, 2, :], ALU.add).then_inc(level, 1)
                    tt(MV[:, :, :, 96:128], c1[:, :, :, :], c2[:, :, :, :], ALU.subtract)
                    reached(5)
                    tt(M[:, :, 64:96], dd[:, :, :], W[:, :, W_DOT:W_CROSS], ALU.mult)
                    for j in range(G):
                        wait(dve, added[b][j], i * 16)
                    tt(slot[b][:, :], move[:, :], keys_c, ALU.add).then_inc(messages[b], 1)

            loop(dve, 0, GROUPS // 2, both)


_WEIGHTS = {
    0: {"skip_s": "L0_gnn_W_skip0", "skip_v": "L0_gnn_W_skip1", "lin_s": "L0_gnn_W_nl0",
        "lin_v": "L0_gnn_W_nl1", "fc1": "L0_gnn_W_fc1", "fc2": "L0_gnn_W_fc2",
        "out_s": "L0_gnn_W_out_s", "out_v": "L0_gnn_W_out_v"},
    1: {"skip_s": "L1_gnn_sc_ws", "skip_v": "L1_gnn_sc_wv", "lin_s": "L1_gnn_lin1_ws",
        "lin_v": "L1_gnn_lin1_wv", "fc1": "L1_gnn_fc_w1", "fc2": "L1_gnn_fc_w2",
        "out_s": "L1_gnn_lin2_ws", "out_v": "L1_gnn_lin2_wv"},
}


def build(nc, t, out):
    ctx = ExitStack()
    with ctx:
        k = allocate(nc, ctx)
        w = {l: {name: t[full] for name, full in _WEIGHTS[l].items()} for l in (0, 1)}
        setup_phase(nc, k, w, t["ea3"], t["attr"])
        node_phase(nc, k, 0, t["x"], None)
        edge_phase(nc, k, 0, t["ef"], t["dst_col"], t["src_col"], t["src_row"], k.rhat)
        node_phase(nc, k, 1, t["x"], k.x1)
        edge_phase(nc, k, 1, t["ef"], t["src_col"], t["dst_col"], t["dst_row"], t["ea4"])
        node_phase(nc, k, 2, k.x1, out)


def kernel(**inputs):
    import concourse.bacc as bacc
    from concourse.bass_utils import run_bass_kernel_spmd

    a = {name: np.asarray(v) for name, v in inputs.items()}

    def by_component(x):
        v = x[:, S_CH:].reshape(-1, V_CH, 3).transpose(0, 2, 1).reshape(-1, 3 * V_CH)
        return np.concatenate([x[:, :S_CH], v], 1)

    def by_tile(e):
        return e.reshape(GROUPS, G, P, -1).transpose(2, 0, 1, 3)

    host = {
        "x": by_component(a["x"]).reshape(P, NT * CH),
        "ef": a["edge_attr_64"].reshape(GROUPS, 2, 4, P, HID).transpose(0, 1, 4, 2, 3).reshape(GROUPS * 128, 4 * P),
        "src_col": by_tile(a["src"]).reshape(P, -1),
        "dst_col": by_tile(a["dst"]).reshape(P, -1),
        "src_row": a["src"].reshape(GROUPS, G * P),
        "dst_row": a["dst"].reshape(GROUPS, G * P),
        "ea3": by_tile(a["edge_attr_3"]).reshape(P, -1),
        "ea4": by_tile(a["edge_attr_4"]).reshape(P, -1),
        "attr": a["node_vec1"].reshape(P, NT),
    }
    for names in _WEIGHTS.values():
        host.update({name: a[name] for name in names.values()})
    nc = bacc.Bacc("TRN2", target_bir_lowering=False, num_devices=1)
    host = {name: np.ascontiguousarray(v) for name, v in host.items()}
    aps = {name: nc.dram_tensor(f"in_{name}", v.shape, mybir.dt.from_np(v.dtype), kind="ExternalInput").ap()
           for name, v in host.items()}
    out = nc.dram_tensor("out", [P, NT * CH], FP32, kind="ExternalOutput").ap()
    build(nc, aps, out)
    r = run_bass_kernel_spmd(nc, [{f"in_{name}": v for name, v in host.items()}], core_ids=[0])
    y = r.results[0]["out"].reshape(NODES, CH)
    v = y[:, S_CH:].reshape(NODES, 3, V_CH).transpose(0, 2, 1).reshape(NODES, 3 * V_CH)
    return np.concatenate([y[:, :S_CH], v], 1)
```

```python
import numpy as np
import concourse.bass as bass
from concourse import mybir
from contextlib import ExitStack

FP32 = mybir.dt.float32
INT32 = mybir.dt.int32
ALU = mybir.AluOpType
ACT = mybir.ActivationFunctionType
AX = mybir.AxisListType

P = 125
NODES = 6250
EDGES = 200000
S_CH, V_CH = 64, 32
CH = S_CH + 3 * V_CH
NT = NODES // P
NB = 5
STEPS = NT // NB
G = 8
GROUPS = EDGES // (P * G)
HID = 64
WCOLS = 224
MSG = 96 + 3 * 128
OUT = 96 + 3 * V_CH
ACCS = 4
ACC_ROWS = NODES + 2 * P
WINDOW = 128
ZERO_PARTS = 6
ZERO_COLS = ACC_ROWS // P * OUT // ZERO_PARTS
MAPS = CH + OUT
BANK = 512
W_SS, W_VV, W_SV, W_DOT, W_CROSS = 0, 64, 96, 160, 192


def bc(ap, axis, n):
    ap = ap.unsqueeze(axis)
    shape = list(ap.shape)
    shape[axis] = n
    return ap.to_broadcast(shape)


def wait(engine, sem, value):
    if not isinstance(value, int) or value > 0:
        engine.wait_ge(sem, value)


def loop(engine, first, end, body, peel=1):
    for i in range(first, first + peel):
        body(i)
    with engine.Fori(first + peel, end) as i:
        body(i)


def exists(i):
    return not isinstance(i, int) or i >= 0


class Phase:
    pass


def allocate(nc, ctx):
    k = Phase()

    def sb(name, shape, dt=FP32):
        return ctx.enter_context(nc.sbuf_tensor(name, shape, dt))

    k.zero = sb("zero", [P, ZERO_COLS])
    k.zeroed = [ctx.enter_context(nc.semaphore(f"zeroed{l}")) for l in (0, 1)]
    k.ident = sb("ident", [128, 128])
    k.earlier = sb("earlier", [P, P])
    k.trash_i = sb("trash_i", [P, 1], INT32)
    k.trash = sb("trash", [P, 1])
    k.attr_c = sb("attr_c", [P, NT])
    k.iota_row = sb("iota_row", [P, WINDOW])
    k.base = sb("base", [128, GROUPS])
    k.rows = sb("rows", [128, GROUPS], INT32)
    k.narrow = sb("narrow", [128, 1], INT32)
    k.maps_a = [sb(f"maps_a{l}", [128, MAPS]) for l in (0, 1)]
    k.maps_b = [sb(f"maps_b{l}", [V_CH, MAPS]) for l in (0, 1)]
    k.fc1 = [sb(f"fc1_{l}", [128, 128]) for l in (0, 1)]
    k.fc2 = [sb(f"fc2_{l}", [128, WCOLS]) for l in (0, 1)]
    k.out_s = [sb(f"out_s{l}", [96, 96]) for l in (0, 1)]
    k.out_v = [sb(f"out_v{l}", [128, V_CH]) for l in (0, 1)]
    k.banks = [ctx.enter_context(nc.psum_tensor(f"bank{n}", [128, BANK], FP32)) for n in range(8)]
    k.table = [nc.dram_tensor(f"table{l}", [NODES, CH], FP32).ap() for l in (0, 1)]
    k.skip = [nc.dram_tensor(f"skip{l}", [P, NT * OUT], FP32).ap() for l in (0, 1)]
    k.x1 = nc.dram_tensor("x1", [P, NT * CH], FP32).ap()
    k.spans = nc.dram_tensor("spans", [GROUPS // 2, 4], FP32).ap()
    k.rhat = nc.dram_tensor("rhat", [P, GROUPS * G * 3], FP32).ap()
    k.acc = [[nc.dram_tensor(f"acc{l}_{n}", [ACC_ROWS, OUT], FP32).ap() for n in range(ACCS)]
             for l in (0, 1)]
    return k


def zero_sums(engine, k, layer):
    for n in range(ACCS):
        view = k.acc[layer][n].rearrange("(p t) c -> p (t c)", p=P)
        for m in range(ZERO_PARTS):
            engine.dma_start(view[:, m * ZERO_COLS:(m + 1) * ZERO_COLS], k.zero[:, :]).then_inc(k.zeroed[layer], 16)


def zeroed(engine, k, layer):
    engine.wait_ge(k.zeroed[layer], 16 * ACCS * ZERO_PARTS)


def setup_phase(nc, k, w, ea3, attr, dst_col):
    ctx = ExitStack()
    with ctx:
        def sb(name, shape, dt=FP32):
            return ctx.enter_context(nc.sbuf_tensor(name, shape, dt))

        def sem(name):
            return ctx.enter_context(nc.semaphore(name))

        CHUNKS = 4
        EC = GROUPS * G // CHUNKS
        ea = sb("ea", [P, CHUNKS, EC * 3])
        sq = sb("sq", [P, EC * 3])
        ss = sb("ss", [P, EC])
        nrm = sb("nrm", [P, EC])
        inv = sb("inv", [P, EC])
        HALF = GROUPS // 2
        dst = sb("dst", [P, GROUPS, G], INT32)
        ends_p = sb("ends_p", [P, 4, HALF])
        ends = sb("ends", [HALF, 4])
        ends_row = sb("ends_row", [128, HALF, 4])
        span = sb("span", [128, GROUPS])
        widest = sb("widest", [128, 1])
        iota_ri = sb("iota_ri", [P, WINDOW], INT32)
        iota_pi = sb("iota_pi", [128, 1], INT32)
        iota_p = sb("iota_p", [128, 1])

        s_cleared, s_zero, s_weights, s_attr = (
            sem("cleared"), sem("zero_ready"), sem("weights"), sem("attr"))
        s_ea = [sem(f"ea_in{c}") for c in range(CHUNKS)]
        s_sum, s_norm, s_step, s_unit, s_stored = (
            sem("sum_sq"), sem("norm"), sem("dve_step"), sem("unit"), sem("rhat_stored"))
        s_filled, s_mask = sem("filled"), sem("masks")
        s_dst, s_ends_p, s_ends_ps, s_ends, s_spans, s_row, s_last = (
            sem("dst_in"), sem("ends_p"), sem("ends_psum"), sem("ends"), sem("spans_out"), sem("ends_row"),
            sem("last"))
        block = ctx.enter_context(nc.Block())

        @block.sync
        def _(sp):
            sp.dma_start(dst[:, :, :].rearrange("p g j -> p (g j)"), dst_col).then_inc(s_dst, 16)
            for c in range(CHUNKS):
                sp.dma_start(ea[:, c, :], ea3[:, c * EC * 3:(c + 1) * EC * 3]).then_inc(s_ea[c], 16)
            sp.dma_start(k.attr_c[:, :], attr).then_inc(s_attr, 16)
            sp.wait_ge(s_cleared, 1)
            n = 0
            for l in (0, 1):
                a, b, fc1, fc2 = k.maps_a[l], k.maps_b[l], k.fc1[l], k.fc2[l]
                t0 = CH + 96
                for to, of in (
                    (a[0:64, 0:64], w[l]["lin_s"]), (a[0:64, CH:CH + 96], w[l]["skip_s"]),
                    (a[64:96, 64:96], w[l]["lin_v"]), (a[96:128, 96:128], w[l]["lin_v"]),
                    (b[:, 128:160], w[l]["lin_v"]),
                    (a[64:96, t0:t0 + 32], w[l]["skip_v"]), (a[96:128, t0 + 32:t0 + 64], w[l]["skip_v"]),
                    (b[:, t0 + 64:t0 + 96], w[l]["skip_v"]),
                    (fc1[0:64, 0:64], w[l]["fc1"]), (fc1[64:128, 64:128], w[l]["fc1"]),
                    (k.out_s[l][:, :], w[l]["out_s"]),
                    (k.out_v[l][:, :], w[l]["out_v"]),
                ):
                    sp.dma_start(to, of).then_inc(s_weights, 16)
                    n += 1
                for half in (0, 64):
                    for to, of, size in ((W_SS, 0, 64), (W_SV, 64, 64), (W_VV, 128, 32),
                                         (W_DOT, 160, 32), (W_CROSS, 192, 32)):
                        sp.dma_start(fc2[half:half + 64, to:to + size],
                                     w[l]["fc2"][:, of:of + size]).then_inc(s_weights, 16)
                        n += 1
            sp.wait_ge(s_ends, 4)
            sp.dma_start(k.spans, ends[:, :]).then_inc(s_spans, 16)
            sp.wait_ge(s_spans, 16)
            sp.dma_start(ends_row[:, :, :].rearrange("p g e -> p (g e)"),
                         k.spans.rearrange("(o g) e -> o (g e)", o=1).to_broadcast([128, 2 * GROUPS])
                         ).then_inc(s_row, 16)
            for c in range(CHUNKS):
                sp.wait_ge(s_unit, c + 1)
                sp.dma_start(k.rhat[:, c * EC * 3:(c + 1) * EC * 3], ea[:, c, :]).then_inc(s_stored, 16)
            sp.wait_ge(s_stored, 16 * CHUNKS)
            sp.wait_ge(s_weights, 16 * n)
            sp.wait_ge(s_attr, 16)

        n_weights = 2 * (12 + 10)

        @block.gpsimd
        def _(pool):
            pool.iota(k.trash_i[:, :], pattern=[[0, 1]], base=NODES, channel_multiplier=1).then_inc(s_mask, 1)
            pool.iota(iota_ri[:, :], pattern=[[1, WINDOW]], base=0, channel_multiplier=0).then_inc(s_mask, 1)
            pool.iota(iota_pi[:, :], pattern=[[0, 1]], base=0, channel_multiplier=1).then_inc(s_mask, 1)
            pool.memset(k.ident[:, :], 0.0).then_inc(s_filled, 1)
            pool.memset(k.earlier[:, :], 1.0).then_inc(s_filled, 1)
            pool.wait_ge(s_filled, 2)
            pool.affine_select(out=k.ident[:, :], in_=k.ident[:, :], compare_op=ALU.not_equal, fill=1.0,
                               base=0, pattern=[[-1, 128]], channel_multiplier=1).then_inc(s_mask, 1)
            pool.affine_select(out=k.earlier[:, :], in_=k.earlier[:, :], compare_op=ALU.is_gt, fill=0.0,
                               base=0, pattern=[[-1, P]], channel_multiplier=1).then_inc(s_mask, 1)
            pool.wait_ge(s_mask, 5)

        @block.scalar
        def _(act):
            act.wait_ge(s_zero, 1)
            zero_sums(act, k, 0)
            for c in range(CHUNKS):
                act.wait_ge(s_sum, c + 1)
                if c:
                    act.wait_ge(s_unit, c)
                nc.scalar.activation(nrm[:, :], ss[:, :], ACT.Sqrt).then_inc(s_norm, 1)

        @block.tensor
        def _(pe):
            pe.wait_ge(s_mask, 5)
            pe.wait_ge(s_ends_p, 4)
            for c in range(4):
                nc.tensor.transpose(k.banks[c][0:HALF, 0:P], ends_p[:, c, :], k.ident[0:P, 0:P]).then_inc(s_ends_ps, 1)

        @block.vector
        def _(dve):
            nc.vector.memset(k.zero[:, :], 0.0).then_inc(s_zero, 1)
            dve.wait_ge(s_dst, 16)
            for c in range(4):
                lo = HALF * (c % 2)
                nc.vector.tensor_reduce(ends_p[:, c, :], dst[:, lo:lo + HALF, :], AX.X,
                                        ALU.min if c < 2 else ALU.max).then_inc(s_ends_p, 1)
            for l in (0, 1):
                for weights in (k.maps_a[l], k.maps_b[l], k.fc1[l]):
                    last = nc.vector.memset(weights[:, :], 0.0)
            last.then_inc(s_cleared, 1)
            steps = 0
            for c in range(CHUNKS):
                v = ea[:, c, :].rearrange("p (e i) -> p e i", i=3)
                dve.wait_ge(s_ea[c], 16)
                nc.vector.tensor_tensor(sq[:, :], ea[:, c, :], ea[:, c, :], ALU.mult).then_inc(s_step, 1)
                dve.wait_ge(s_step, 2 * c + 1)
                nc.vector.tensor_reduce(ss[:, :], sq[:, :].rearrange("p (e i) -> p e i", i=3), AX.X,
                                        ALU.add).then_inc(s_sum, 1)
                dve.wait_ge(s_norm, c + 1)
                nc.vector.reciprocal(inv[:, :], nrm[:, :]).then_inc(s_step, 1)
                dve.wait_ge(s_step, 2 * c + 2)
                nc.vector.tensor_tensor(v, v, bc(inv[:, :], 2, 3), ALU.mult).then_inc(s_unit, 1)
            dve.wait_ge(s_mask, 5)
            nc.vector.tensor_copy(k.trash[:, :], k.trash_i[:, :])
            nc.vector.tensor_copy(k.iota_row[:, :], iota_ri[:, :])
            nc.vector.tensor_copy(iota_p[:, :], iota_pi[:, :]).then_inc(s_last, 1)
            for c in range(4):
                dve.wait_ge(s_ends_ps, c + 1)
                nc.vector.tensor_reduce(ends[:, c:c + 1], k.banks[c][0:HALF, 0:P], AX.X,
                                        ALU.min if c < 2 else ALU.max).then_inc(s_ends, 1)
            dve.wait_ge(s_row, 16)
            dve.wait_ge(s_last, 1)
            by_half = ends_row[:, :, :].rearrange("p g e -> p e g")
            least, greatest = by_half[:, 0:2, :], by_half[:, 2:4, :]

            def halves(x):
                return x[:, :].rearrange("p (h g) -> p h g", h=2)

            nc.vector.tensor_copy(halves(k.base), least)
            nc.vector.tensor_scalar(halves(k.rows), least, iota_p[:, 0:1], None, ALU.add)
            nc.vector.tensor_tensor(halves(span), greatest, least,
                                    ALU.subtract).then_inc(s_last, 1)
            dve.wait_ge(s_last, 2)
            nc.vector.tensor_reduce(widest[:, :], span[:, :], AX.X, ALU.max).then_inc(s_last, 1)
            dve.wait_ge(s_last, 3)
            nc.vector.tensor_scalar(k.narrow[:, :], widest[:, :], float(WINDOW), None, ALU.is_lt)
            dve.wait_ge(s_weights, 16 * n_weights)
            r2, r3 = 2.0 ** -0.5, 3.0 ** -0.5
            common1 = (1.0 / HID ** 0.5) * 16.0 ** -0.5
            cs, cv = common1 * 96.0 ** -0.5, common1 * 128.0 ** -0.5
            for weights, lo, hi, factor in (
                (k.out_s[0], 0, 96, 1 / 32.0),
                (k.out_v[0], 0, 64, 3.0 ** 0.5 / 32), (k.out_v[0], 64, 96, 1 / 32.0),
                (k.out_v[0], 96, 128, 3.0 ** 0.5 * r2 / 32),
                (k.maps_a[1], 0, 64, S_CH ** -0.5), (k.maps_a[1], 64, 128, V_CH ** -0.5),
                (k.maps_b[1], 0, 32, V_CH ** -0.5),
                (k.out_s[1], 0, 64, cs), (k.out_s[1], 64, 96, cs * r3),
                (k.out_v[1], 0, 64, cv), (k.out_v[1], 64, 96, cv), (k.out_v[1], 96, 128, cv * r2),
            ):
                part = weights[lo:hi, :]
                nc.vector.tensor_scalar(part, part, factor, None, ALU.mult)


def node_phase(nc, k, phase, x_in, x_out):
    combine, project = phase > 0, phase < 2
    ctx = ExitStack()
    with ctx:
        def sb(name, shape, dt=FP32):
            return ctx.enter_context(nc.sbuf_tensor(f"nodes{phase}_{name}", shape, dt))

        def sem(name):
            return ctx.enter_context(nc.semaphore(f"n{phase}_{name}"))

        x = [sb(f"x{b}", [P, NB, CH]) for b in (0, 1)]
        if combine:
            acc = [sb(f"acc{b}", [P, ACCS, NB, OUT]) for b in (0, 1)]
            skip_in = [sb(f"skip_in{b}", [P, NB, OUT]) for b in (0, 1)]
            gate = sb("gate", [P, NB, 96])
            y = sb("y", [P, NB, CH])
            x1 = sb("sum", [P, NB, CH])
        if project:
            cent = sb("cent", [P, NB, CH])
            square = sb("square", [P, NB, CH])
            sum_x, mean, sum_sq, var, std, rstd = (
                sb(name, [P, NB]) for name in ("sum_x", "mean", "sum_sq", "var", "std", "rstd"))
            h = sb("h", [P, NB, CH])
            hT_a = sb("hT_a", [128, NB, P])
            hT_b = sb("hT_b", [V_CH, NB, P])
            maps = sb("maps", [P, NB, MAPS])
            maps_a, maps_b = k.maps_a[phase], k.maps_b[phase]
        in_dma = [sem(f"in_dma{b}") for b in (0, 1)]
        dve_done, gated, std_ready = sem("dve_done"), sem("gated"), sem("std_ready")
        x1_stored, table_stored, skip_stored = sem("x1_stored"), sem("table_stored"), sem("skip_stored")
        transposed, hT_ready, mapped, maps_ready = (
            sem("transposed"), sem("hT_ready"), sem("mapped"), sem("maps_ready"))
        LOADS = 1 + (ACCS + 1 if combine else 0)
        last = phase - 1

        order = (["pairs", "halves", "pre", "scaled", "scalars", "vectors", "x1"] if combine else []) + (
            ["sum_x", "mean", "cent", "square", "sum_sq", "var", "rstd", "h"] if project else [])
        if phase == 1:
            order.remove("scaled")

        def upto(n, name):
            return n * len(order) + (order.index(name) + 1)

        PRE = "scaled" if phase == 2 else "pre"
        IN_USED = "x1" if combine else "cent"
        block = ctx.enter_context(nc.Block())

        @block.sync
        def _(sp):
            def load(n, b):
                sp.dma_start(x[b][:, :, :].rearrange("p t c -> p (t c)"),
                             x_in[:, bass.ds(n * (NB * CH), NB * CH)]).then_inc(in_dma[b], 16)
                if combine:
                    sp.dma_start(skip_in[b][:, :, :].rearrange("p t c -> p (t c)"),
                                 k.skip[last][:, bass.ds(n * (NB * OUT), NB * OUT)]).then_inc(in_dma[b], 16)
                    for a in range(ACCS):
                        sums = k.acc[last][a][0:NODES, :].rearrange("(p t) c -> p (t c)", p=P)
                        sp.dma_start(acc[b][:, a, :, :].rearrange("p t c -> p (t c)"),
                                     sums[:, bass.ds(n * (NB * OUT), NB * OUT)]).then_inc(in_dma[b], 16)

            load(0, 0)
            load(1, 1)
            with sp.Fori(1, STEPS // 2) as i:
                for b in (0, 1):
                    wait(sp, dve_done, upto(i * 2 + (b - 2), IN_USED))
                    load(i * 2 + b, b)
            if phase == 0:
                zeroed(sp, k, 0)
            if phase == 1:
                zeroed(sp, k, 1)

        @block.vector
        def _(dve):
            def both(i):
                for b in (0, 1):
                    n = i * 2 + b
                    src = x1 if combine else x[b]
                    wait(dve, in_dma[b], (i + 1) * (16 * LOADS))
                    if combine:
                        A, pre, sk = acc[b], acc[b][:, 0, :, :], skip_in[b]
                        nc.vector.tensor_tensor(A[:, 0:2, :, :].rearrange("p a t c -> p (a t c)"),
                                                A[:, 0:2, :, :].rearrange("p a t c -> p (a t c)"),
                                                A[:, 2:4, :, :].rearrange("p a t c -> p (a t c)"),
                                                ALU.add).then_inc(dve_done, 1)
                        wait(dve, dve_done, upto(n, "pairs"))
                        nc.vector.tensor_tensor(pre, pre, A[:, 1, :, :], ALU.add).then_inc(dve_done, 1)
                        wait(dve, dve_done, upto(n, "halves"))
                        nc.vector.tensor_tensor(pre, pre, sk[:, :, :], ALU.add).then_inc(dve_done, 1)
                        wait(dve, dve_done, upto(n, "pre"))
                        if phase == 2:
                            nc.vector.tensor_tensor(
                                pre, pre, bc(k.attr_c[:, bass.ds(n * NB, NB)], 2, OUT),
                                ALU.mult).then_inc(dve_done, 1)
                        wait(dve, gated, n + 1)
                        nc.vector.tensor_tensor(y[:, :, 0:S_CH], pre[:, :, 0:S_CH], gate[:, :, 0:S_CH],
                                                ALU.mult).then_inc(dve_done, 1)
                        for c in range(3):
                            lo = S_CH + V_CH * c
                            ins = nc.vector.tensor_tensor(
                                y[:, :, lo:lo + V_CH], pre[:, :, 96 + V_CH * c:96 + V_CH * (c + 1)],
                                gate[:, :, S_CH:96], ALU.mult)
                        ins.then_inc(dve_done, 1)
                        wait(dve, dve_done, upto(n, "vectors"))
                        wait(dve, x1_stored, n * 16)
                        nc.vector.tensor_tensor(x1[:, :, :], x[b][:, :, :], y[:, :, :],
                                                ALU.add).then_inc(dve_done, 1)
                        wait(dve, dve_done, upto(n, "x1"))
                    if project:
                        nc.vector.tensor_reduce(sum_x[:, :], src[:, :, :], AX.X, ALU.add).then_inc(dve_done, 1)
                        wait(dve, dve_done, upto(n, "sum_x"))
                        nc.vector.tensor_scalar(mean[:, :], sum_x[:, :], 1.0 / CH, None,
                                                ALU.mult).then_inc(dve_done, 1)
                        wait(dve, dve_done, upto(n, "mean"))
                        nc.vector.tensor_tensor(cent[:, :, :], src[:, :, :], bc(mean[:, :], 2, CH),
                                                ALU.subtract).then_inc(dve_done, 1)
                        wait(dve, dve_done, upto(n, "cent"))
                        nc.vector.tensor_tensor(square[:, :, :], cent[:, :, :], cent[:, :, :],
                                                ALU.mult).then_inc(dve_done, 1)
                        wait(dve, dve_done, upto(n, "square"))
                        nc.vector.tensor_reduce(sum_sq[:, :], square[:, :, :], AX.X, ALU.add).then_inc(dve_done, 1)
                        wait(dve, dve_done, upto(n, "sum_sq"))
                        nc.vector.tensor_scalar(var[:, :], sum_sq[:, :], 1.0 / CH, 1e-5, ALU.mult,
                                                ALU.add).then_inc(dve_done, 1)
                        wait(dve, std_ready, n + 1)
                        nc.vector.reciprocal(rstd[:, :], std[:, :]).then_inc(dve_done, 1)
                        wait(dve, dve_done, upto(n, "rstd"))
                        wait(dve, transposed, n)
                        nc.vector.scalar_tensor_tensor(h[:, :, :], cent[:, :, :], 0.0, bc(rstd[:, :], 2, CH),
                                                       ALU.max, ALU.mult).then_inc(dve_done, 1)

            loop(dve, 0, STEPS // 2, both)

        @block.scalar
        def _(act):
            def transposed_out(n):
                wait(act, transposed, n + 1)
                for to, of, rows in ((hT_a, 0, 128), (hT_b, 2, V_CH)):
                    nc.scalar.activation(
                        to[:, 0:4, :].rearrange("r t p -> r (t p)"),
                        k.banks[of][0:rows, 0:4 * P], ACT.Copy).then_inc(hT_ready, 1)
                nc.scalar.activation(hT_a[:, 4, :], k.banks[1][:, 0:P], ACT.Copy).then_inc(hT_ready, 1)
                nc.scalar.activation(hT_b[:, 4, :], k.banks[1][0:V_CH, P:2 * P],
                                     ACT.Copy).then_inc(hT_ready, 1)

            def maps_out(n):
                wait(act, table_stored, n * 16)
                wait(act, skip_stored, n * 16)
                for t in range(NB):
                    wait(act, mapped, n * NB + (t + 1))
                    bank = k.banks[3 + t]
                    if phase == 1:
                        nc.scalar.activation(maps[:, t, 0:CH], bank[0:P, 0:CH], ACT.Copy,
                                             scale=k.attr_c[:, bass.ds(n * NB + t, 1)])
                        nc.scalar.activation(maps[:, t, CH:MAPS], bank[0:P, CH:MAPS],
                                             ACT.Copy).then_inc(maps_ready, 1)
                    else:
                        nc.scalar.activation(maps[:, t, :], bank[0:P, 0:MAPS],
                                             ACT.Copy).then_inc(maps_ready, 1)
                wait(act, maps_ready, (n + 1) * NB)
                rows = k.table[phase].rearrange("(p t) c -> p t c", p=P)
                act.dma_start(rows[:, bass.ds(n * NB, NB), :], maps[:, :, 0:CH]).then_inc(table_stored, 16)
                rows = k.skip[phase].rearrange("p (t c) -> p t c", c=OUT)
                act.dma_start(rows[:, bass.ds(n * NB, NB), :], maps[:, :, CH:MAPS]).then_inc(skip_stored, 16)

            def both(i):
                for b in (0, 1):
                    n = i * 2 + b
                    has_before = project and exists(n - 1)
                    if has_before:
                        transposed_out(n - 1)
                    if combine:
                        wait(act, dve_done, upto(n, PRE))
                        nc.scalar.activation(gate[:, :, :], acc[b][:, 0, :, 0:96], ACT.Sigmoid).then_inc(gated, 1)
                        wait(act, dve_done, upto(n, "x1"))
                        act.dma_start(x_out[:, bass.ds(n * (NB * CH), NB * CH)],
                                      x1[:, :, :].rearrange("p t c -> p (t c)")).then_inc(x1_stored, 16)
                    if project:
                        wait(act, dve_done, upto(n, "var"))
                        nc.scalar.activation(std[:, :], var[:, :], ACT.Sqrt).then_inc(std_ready, 1)
                    if has_before:
                        maps_out(n - 1)

            loop(act, 0, STEPS // 2, both)
            if project:
                transposed_out(STEPS - 1)
                maps_out(STEPS - 1)
            if combine:
                wait(act, x1_stored, STEPS * 16)
            if project:
                wait(act, table_stored, STEPS * 16)
                wait(act, skip_stored, STEPS * 16)

        if project:
            @block.tensor
            def _(pe):
                def step(n):
                    wait(pe, dve_done, upto(n, "h"))
                    wait(pe, hT_ready, n * 4)
                    for t in range(NB):
                        bank, col = (0, t * P) if t < 4 else (1, 0)
                        nc.tensor.transpose(k.banks[bank][:, col:col + P], h[:, t, 0:128], k.ident[0:P, 0:P])
                        bank, col = (2, t * P) if t < 4 else (1, P)
                        ins = nc.tensor.transpose(k.banks[bank][0:V_CH, col:col + P], h[:, t, 128:CH],
                                                  k.ident[0:P, 0:P])
                    ins.then_inc(transposed, 1)
                    wait(pe, hT_ready, (n + 1) * 4)
                    wait(pe, maps_ready, n * NB)
                    for t in range(NB):
                        out = k.banks[3 + t][0:P, 0:MAPS]
                        nc.tensor.matmul(out, hT_a[:, t, :], maps_a[:, :], start=True, stop=False)
                        nc.tensor.matmul(out, hT_b[:, t, :], maps_b[:, :], start=False,
                                         stop=True).then_inc(mapped, 1)

                loop(pe, 0, STEPS, step)


def edge_phase(nc, k, layer, ef, idx, keycol, keys, vec, e0=None):
    ctx = ExitStack()
    with ctx:
        def sb(name, shape, dt=FP32):
            return ctx.enter_context(nc.sbuf_tensor(f"e{layer}_{name}", shape, dt))

        def two(name, shape, dt=FP32):
            return [sb(f"{name}{b}", shape, dt) for b in (0, 1)]

        def sem(name):
            return ctx.enter_context(nc.semaphore(f"e{layer}_{name}"))

        def sems(name, n=2):
            return [sem(f"{name}{m}") for m in range(n)]

        ef_in = two("ef", [128, 4 * P])
        idx_in = two("idx", [P, G], INT32)
        key_in = two("key", [P, G], INT32)
        keyrow = two("keyrow", [P, G, P], INT32)
        vec_in = two("vec", [P, G, 3])
        hid = two("hid", [128, 4 * P])
        wts = two("wts", [P, G, WCOLS])
        xg = two("xg", [P, G, CH])
        msg = two("msg", [P, G, MSG])
        same_in = two("same", [P, G, WINDOW])
        slot = two("slot", [P, G], INT32)
        outs = two("outs", [P, G, OUT])
        if layer == 1:
            e0_all = sb("e0_all", [P, GROUPS * G])
        qs = two("q", [P, G, S_CH])
        y = sb("y", [P, G, 3, V_CH])
        d = sb("d", [P, G, 3, V_CH])
        dd = sb("dd", [P, G, V_CH])
        cross = sb("cross", [P, G, 6, V_CH])
        masked = sb("masked", [P, G, P])
        count = sb("count", [P, G])
        away = sb("away", [P, G])
        move = sb("move", [P, G])
        aggT = two("aggT", [128, 4, P])
        fc1, fc2 = k.fc1[layer], k.fc2[layer]
        out_s, out_v = k.out_s[layer], k.out_v[layer]

        same = [x[:, :, :].rearrange("p g e -> p (g e)")[:, 0:G * P].rearrange("p (g e) -> p g e", e=P)
                for x in same_in]
        agg_sb = two("agg_sb", [128, MSG])
        winT = two("winT", [128, 4, WINDOW])
        win_outs = two("win_outs", [WINDOW, OUT])
        row_in = two("row_in", [WINDOW, 1], INT32)
        relative = sb("relative", [P, G])
        hid_ps = k.banks[0]
        w_ps, agg_ps, out_ps = k.banks[1:3], k.banks[3:5], k.banks[5:7]
        win_T_ps, win_out_ps = k.banks[5], k.banks[6]

        indexed, features, loaded, gathered = sems("indexed"), sems("features"), sems("loaded"), sems("gathered")
        hid_psum, hid_ready = sems("hid_psum"), sems("hid_ready")
        messages, summed = sems("messages"), sems("summed")
        w_psum, w_ready = sems("w_psum"), sems("w_ready")
        agg_psum, agg_ready = sems("agg_psum"), sems("agg_ready")
        out_psum, out_ready = sems("out_psum"), sems("out_ready")
        added = [sems(f"added{b}_", G) for b in (0, 1)]
        passed = sem("passed")
        mapped_T, win_aggT = agg_psum, agg_ready
        mapped_out, win_out = out_psum, out_ready
        win_added = [added[0][0], added[1][0]]
        win_agg = [added[0][1], added[1][1]]
        win_rows = [added[0][2], added[1][2]]
        q_ready = [added[0][3], added[1][3]]
        spread = [added[0][4], added[1][4]]
        if layer == 1:
            e0_in = sem("e0_in")
        level = sem("level")
        LAST = GROUPS // 2 - 1
        LEVELS = 5
        block = ctx.enter_context(nc.Block())

        def choose(engine, program):
            if layer == 0:
                program(False)
                return
            narrow = engine.value_load(k.narrow[0:1, 0:1], min_val=0, max_val=1)
            with engine.If(narrow):
                program(True)
            with engine.Else():
                program(False)

        def nth(i, b, q):
            return i * 4 + (2 * b + q // 2)

        def nth_tile(i, b, j):
            return i * 8 + (4 * b + j // 2)

        @block.sync
        def _(sp):
            def program(windowed):
                def load_early(i, b):
                    g = i * 2 + b
                    wait(sp, gathered[b], i * (16 * G))
                    sp.dma_start(idx_in[b][:, :], idx[:, bass.ds(g * G, G)]).then_inc(indexed[b], 16)
                    wait(sp, hid_psum[b], i)
                    sp.dma_start(ef_in[b][:, :], ef[bass.ds(g * 128, 128), :]).then_inc(features[b], 16)

                def load_late(i, b):
                    g = i * 2 + b
                    wait(sp, messages[b], i)
                    if windowed:
                        wait(sp, spread[b], i)
                    sp.dma_start(key_in[b][:, :], keycol[:, bass.ds(g * G, G)]).then_inc(loaded[b], 16)
                    sp.dma_start(vec_in[b][:, :, :].rearrange("p g a -> p (g a)"),
                                 vec[:, bass.ds(g * (G * 3), G * 3)]).then_inc(loaded[b], 16)
                    if not windowed:
                        row = keys[bass.ds(g, 1), :].to_broadcast([P, G * P])
                        sp.dma_start(keyrow[b][:, :, :].rearrange("p g e -> p (g e)"), row).then_inc(loaded[b], 16)

                def both(i):
                    load_late(i, 0)
                    load_early(i, 1)
                    load_late(i, 1)
                    load_early(i + 1, 0)

                load_early(0, 0)
                if layer == 1:
                    sp.dma_start(e0_all[:, :], e0).then_inc(e0_in, 16)
                if layer == 0:
                    zero_sums(sp, k, 1)
                loop(sp, 0, LAST, both)
                load_late(LAST, 0)
                load_early(LAST, 1)
                load_late(LAST, 1)

            choose(sp, program)

        @block.gpsimd
        def _(pool):
            def program(windowed):
                def gather(i, b, j):
                    pool.indirect_dma_start(xg[b][:, j, :], None, k.table[layer],
                                            bass.IndirectOffsetOnAxis(ap=idx_in[b][:, j:j + 1], axis=0)
                                            ).then_inc(gathered[b], 16)

                def before_gathers(i, b):
                    wait(pool, indexed[b], (i + 1) * 16)
                    wait(pool, messages[b], i)
                    pool.sem_inc(passed, 1)

                def scatter(i, b, j):
                    if j % 2 == 0:
                        wait(pool, out_ready[(j // 2) % 2], nth(i, b, j // 2) + 1)
                    if j >= ACCS:
                        wait(pool, added[b][j - ACCS], (i + 1) * 16)
                    elif b:
                        wait(pool, added[0][j + G - ACCS], (i + 1) * 16)
                    else:
                        wait(pool, added[1][j + G - ACCS], i * 16)
                    pool.sem_inc(passed, 1)
                    pool.indirect_dma_start(k.acc[layer][j % ACCS],
                                            bass.IndirectOffsetOnAxis(ap=slot[b][:, j:j + 1], axis=0),
                                            outs[b][:, j, :], None, compute_op=ALU.add).then_inc(added[b][j], 16)

                def scatter_window(i, b):
                    wait(pool, win_out[b], i + 1)
                    wait(pool, win_added[b], i * 16)
                    pool.sem_inc(passed, 1)
                    pool.tensor_copy(row_in[b][:, :],
                                     k.rows[:, bass.ds(i * 2 + b, 1)]).then_inc(win_rows[b], 1)
                    wait(pool, win_rows[b], i + 1)
                    pool.sem_inc(passed, 1)
                    pool.indirect_dma_start(k.acc[layer][b],
                                            bass.IndirectOffsetOnAxis(ap=row_in[b][:, 0:1], axis=0),
                                            win_outs[b][:, :], None, compute_op=ALU.add).then_inc(win_added[b], 16)

                for b in (0, 1):
                    before_gathers(0, b)
                    for j in range(G):
                        gather(0, b, j)
                def both(i):
                    for b in (0, 1):
                        before_gathers(i, b)
                        for j in range(G):
                            gather(i, b, j)
                            if not windowed:
                                scatter(i - 1, b, j)
                        if windowed and exists(i - 2):
                            scatter_window(i - 2, b)

                loop(pool, 1, LAST + 1, both, peel=2 if windowed else 1)
                if windowed:
                    for i in (LAST - 1, LAST):
                        for b in (0, 1):
                            scatter_window(i, b)
                    for b in (0, 1):
                        wait(pool, win_added[b], (LAST + 1) * 16)
                    return
                for b in (0, 1):
                    for j in range(G):
                        scatter(LAST, b, j)
                for b in (0, 1):
                    for j in range(G):
                        wait(pool, added[b][j], (LAST + 1) * 16)

            choose(pool, program)

        @block.tensor
        def _(pe):
            def program(windowed):
                def fc1_of(i, b):
                    wait(pe, features[b], (i + 1) * 16)
                    wait(pe, hid_ready[1 - b], i + b)
                    nc.tensor.matmul(hid_ps[:, 0:4 * P], fc1[:, :], ef_in[b][:, :], start=True,
                                     stop=True).then_inc(hid_psum[b], 1)

                def weights(i, b, q):
                    if q == 0:
                        wait(pe, hid_ready[b], i + 1)
                    wait(pe, w_ready[q % 2], nth(i, b, q))
                    half = 64 * (q // 2)
                    for j in (0, 1):
                        cols = (2 * (q % 2) + j) * P
                        ins = nc.tensor.matmul(w_ps[q % 2][0:P, j * WCOLS:(j + 1) * WCOLS],
                                               hid[b][half:half + 64, cols:cols + P], fc2[half:half + 64, :],
                                               start=True, stop=True)
                    ins.then_inc(w_psum[q % 2], 1)

                def agg(i, b, j):
                    if j == 0:
                        wait(pe, messages[b], i + 1)
                    wait(pe, agg_ready[j % 2], nth_tile(i, b, j))
                    for c in range(4):
                        lo = 0 if c == 0 else 96 + 128 * (c - 1)
                        ins = nc.tensor.matmul(agg_ps[j % 2][:, c * P:(c + 1) * P], msg[b][:, j, lo:lo + 128],
                                               same[b][:, j, :], start=True, stop=True)
                    ins.then_inc(agg_psum[j % 2], 1)

                def mapped(i, b, j):
                    q = j // 2
                    wait(pe, agg_ready[j % 2], nth_tile(i, b, j) + 1)
                    if j % 2 == 0:
                        wait(pe, out_ready[q % 2], nth(i, b, q))
                    col = (j % 2) * OUT
                    to = out_ps[q % 2]
                    ins = nc.tensor.matmul(to[0:P, col:col + 96], aggT[j % 2][0:96, 0, :], out_s[:, :],
                                           start=True, stop=True)
                    if j == G - 1:
                        ins.then_inc(summed[b], 1)
                    for c in range(3):
                        lo = col + 96 + V_CH * c
                        ins = nc.tensor.matmul(to[0:P, lo:lo + V_CH], aggT[j % 2][:, 1 + c, :], out_v[:, :],
                                               start=True, stop=True)
                    if j % 2:
                        ins.then_inc(out_psum[q % 2], 1)

                def agg_window(i, b, j):
                    if j == 0:
                        wait(pe, messages[b], i + 1)
                        wait(pe, spread[b], i + 1)
                        wait(pe, win_agg[b], i)
                    ins = nc.tensor.matmul(agg_ps[b][:, 0:MSG], same_in[b][:, j, :], msg[b][:, j, :],
                                           start=j == 0, stop=j == G - 1)
                    if j == G - 1:
                        ins.then_inc(summed[b], 1)

                def transposes(i, b):
                    wait(pe, win_agg[b], i + 1)
                    wait(pe, win_aggT[1 - b], i + b)
                    for c in range(4):
                        lo = 0 if c == 0 else 96 + 128 * (c - 1)
                        ins = nc.tensor.transpose(win_T_ps[:, c * WINDOW:(c + 1) * WINDOW],
                                                  agg_sb[b][:, lo:lo + 128], k.ident[:, :])
                    ins.then_inc(mapped_T[b], 1)

                def map_window(i, b):
                    wait(pe, win_aggT[b], i + 1)
                    wait(pe, win_out[1 - b], i + b)
                    nc.tensor.matmul(win_out_ps[:, 0:96], winT[b][0:96, 0, :], out_s[:, :],
                                     start=True, stop=True)
                    for c in range(3):
                        lo = 96 + V_CH * c
                        ins = nc.tensor.matmul(win_out_ps[:, lo:lo + V_CH], winT[b][:, 1 + c, :], out_v[:, :],
                                               start=True, stop=True)
                    ins.then_inc(mapped_out[b], 1)

                def windows(i, b, next_weights):
                    before = (i, 0) if b else (i - 1, 1)
                    for j in range(G):
                        agg_window(i, b, j)
                        if j % 2:
                            next_weights(j // 2)
                        if j == 2 and exists(before[0]):
                            transposes(*before)
                        if j == 5 and exists(before[0]):
                            map_window(*before)

                for b in (0, 1):
                    fc1_of(0, b)
                    for q in range(4):
                        weights(0, b, q)
                def both(i):
                    for b in (0, 1):
                        fc1_of(i, b)
                        if windowed:
                            windows(i - 1, b, lambda q: weights(i, b, q))
                            continue
                        for j in range(G):
                            agg(i - 1, b, j)
                            if j:
                                mapped(i - 1, b, j - 1)
                            if j % 2:
                                weights(i, b, j // 2)
                        mapped(i - 1, b, G - 1)

                loop(pe, 1, LAST + 1, both)
                if windowed:
                    for b in (0, 1):
                        windows(LAST, b, lambda q: None)
                    transposes(LAST, 1)
                    map_window(LAST, 1)
                    return
                for b in (0, 1):
                    for j in range(G):
                        agg(LAST, b, j)
                        if j:
                            mapped(LAST, b, j - 1)
                    mapped(LAST, b, G - 1)

            choose(pe, program)

        @block.scalar
        def _(act):
            def program(windowed):
                def hidden(i, b):
                    wait(act, hid_psum[b], i + 1)
                    if layer == 0:
                        nc.scalar.activation(hid[b][:, :], hid_ps[:, 0:4 * P], ACT.Relu).then_inc(hid_ready[b], 1)
                    else:
                        nc.scalar.activation(hid[b][:, :], hid_ps[:, 0:4 * P], ACT.Silu,
                                             scale=HID ** -0.5).then_inc(hid_ready[b], 1)

                def weights(i, b, q):
                    if q == 0:
                        wait(act, messages[b], i)
                    wait(act, w_psum[q % 2], nth(i, b, q) + 1)
                    to = wts[b][:, 2 * q:2 * q + 2, :]
                    of = w_ps[q % 2][0:P, 0:2 * WCOLS].rearrange("p (j w) -> p j w", j=2)
                    if layer == 1:
                        for j in (0, 1):
                            nc.scalar.activation(to[:, j, 0:W_SV], of[:, j, 0:W_SV], ACT.Copy,
                                                 scale=e0_all[:, bass.ds((i * 2 + b) * G + (2 * q + j), 1)])
                        to, of = to[:, :, W_SV:WCOLS], of[:, :, W_SV:WCOLS]
                    nc.scalar.activation(to, of, ACT.Copy).then_inc(w_ready[q % 2], 1)

                def spread_q(i, b, tiles):
                    if 0 in tiles:
                        wait(act, q_ready[b], i + 1)
                    for j in tiles:
                        for c in range(3):
                            lo = 96 + 128 * c
                            ins = nc.scalar.activation(msg[b][:, j, lo:lo + S_CH], qs[b][:, j, :], ACT.Copy,
                                                       scale=vec_in[b][:, j, c:c + 1])
                    if G - 1 in tiles:
                        ins.then_inc(spread[b], 1)

                def agg(i, b, j):
                    wait(act, agg_psum[j % 2], nth_tile(i, b, j) + 1)
                    nc.scalar.activation(aggT[j % 2][:, :, :].rearrange("c m e -> c (m e)"),
                                         agg_ps[j % 2][:, 0:4 * P], ACT.Copy).then_inc(agg_ready[j % 2], 1)

                def pair_out(i, b, q):
                    wait(act, out_psum[q % 2], nth(i, b, q) + 1)
                    wait(act, added[b][2 * q], i * 16)
                    wait(act, added[b][2 * q + 1], i * 16)
                    nc.scalar.activation(outs[b][:, 2 * q:2 * q + 2, :].rearrange("p j c -> p (j c)"),
                                         out_ps[q % 2][0:P, 0:2 * OUT], ACT.Copy).then_inc(out_ready[q % 2], 1)

                def window_steps(i, b):
                    def sums_out():
                        wait(act, summed[b], i + 1)
                        nc.scalar.activation(agg_sb[b][:, :], agg_ps[b][:, 0:MSG], ACT.Copy).then_inc(win_agg[b], 1)

                    def transposed_out():
                        wait(act, mapped_T[b], i + 1)
                        nc.scalar.activation(winT[b][:, :, :].rearrange("c m e -> c (m e)"), win_T_ps[:, :],
                                             ACT.Copy).then_inc(win_aggT[b], 1)

                    def rows_out():
                        wait(act, mapped_out[b], i + 1)
                        wait(act, win_added[b], i * 16)
                        nc.scalar.activation(win_outs[b][:, :], win_out_ps[:, 0:OUT],
                                             ACT.Copy).then_inc(win_out[b], 1)

                    return sums_out, transposed_out, rows_out

                def windows(i, b, next_weights, next_spread=True):
                    before = (i, 0) if b else (i - 1, 1)
                    after = (i + 1, 0) if b else (i, 1)
                    moves = window_steps(*before) if exists(before[0]) else ()
                    for q in range(4):
                        if q in (0, 1, 3) and moves:
                            moves[(0, 1, None, 2)[q]]()
                        next_weights(q)
                        if q < 3 and next_spread:
                            spread_q(*after, range(G)[3 * q:3 * q + 3])

                def sums(i, b, next_weights):
                    for j in range(G):
                        agg(i, b, j)
                        if j and j % 2 == 0:
                            pair_out(i, b, j // 2 - 1)
                        if j % 2:
                            next_weights(j // 2)
                    pair_out(i, b, G // 2 - 1)

                if layer == 1:
                    wait(act, e0_in, 16)
                for b in (0, 1):
                    hidden(0, b)
                    for q in range(4):
                        weights(0, b, q)
                if windowed:
                    spread_q(0, 0, range(G))
                def both(i):
                    for b in (0, 1):
                        hidden(i, b)
                        (windows if windowed else sums)(i - 1, b, lambda q: weights(i, b, q))

                loop(act, 1, LAST + 1, both, peel=2 if windowed else 1)
                if windowed:
                    windows(LAST, 0, lambda q: None)
                    windows(LAST, 1, lambda q: None, next_spread=False)
                    for move in window_steps(LAST, 1):
                        move()
                    return
                for b in (0, 1):
                    sums(LAST, b, lambda q: None)

            choose(act, program)

        @block.vector
        def _(dve):
            def program(windowed):
                def both(i):
                    for b in (0, 1):
                        n = i * 2 + b
                        tt = nc.vector.tensor_tensor

                        def reached(l):
                            wait(dve, level, n * LEVELS + l)

                        W, X, M, S = wts[b], xg[b], msg[b], same[b]
                        V = X[:, :, S_CH:CH].rearrange("p g (c m) -> p g c m", c=3)
                        MV = M[:, :, 96:MSG].rearrange("p g (c m) -> p g c m", c=3)
                        keys_c, e = key_in[b][:, :], vec_in[b]

                        wait(dve, loaded[b], (i + 1) * (32 if windowed else 48))
                        wait(dve, summed[b], i)
                        if windowed:
                            nc.vector.tensor_scalar(relative[:, :], keys_c, k.base[0:P, bass.ds(n, 1)], None,
                                                    ALU.subtract).then_inc(level, 1)
                            reached(1)
                            tt(same_in[b][:, :, :], bc(k.iota_row[:, :], 1, G), bc(relative[:, :], 2, WINDOW),
                               ALU.is_equal).then_inc(level, 1)
                        else:
                            tt(S[:, :, :], keyrow[b][:, :, :], bc(keys_c, 2, P), ALU.is_equal).then_inc(level, 1)
                            reached(1)
                            for j in range(G):
                                nc.vector.tensor_tensor_reduce(
                                    out=masked[:, j, :], in0=S[:, j, :], in1=k.earlier[:, :], scale=1.0,
                                    scalar=0.0, op0=ALU.mult, op1=ALU.add, accum_out=count[:, j:j + 1])
                            nc.vector.tensor_scalar(away[:, :], keys_c, -1.0, k.trash[:, 0:1],
                                                    ALU.mult, ALU.add).then_inc(level, 1)
                        for bank in (0, 1):
                            wait(dve, w_ready[bank], nth(i, b, 2) + 1)
                        wait(dve, gathered[b], (i + 1) * (16 * G))
                        reached(2)
                        ins = tt(qs[b][:, :, :], W[:, :, W_SV:W_DOT], X[:, :, 0:S_CH], ALU.mult)
                        if windowed:
                            ins.then_inc(q_ready[b], 1)
                        tt(d[:, :, :, :], V, bc(e[:, :, :], 3, V_CH), ALU.mult)
                        tt(y[:, :, :, :], V, bc(W[:, :, W_CROSS:WCOLS], 2, 3), ALU.mult)
                        tt(M[:, :, 0:S_CH], W[:, :, W_SS:W_VV], X[:, :, 0:S_CH], ALU.mult)
                        ins = tt(MV[:, :, :, 64:96], V, bc(W[:, :, W_VV:W_SV], 2, 3), ALU.mult)
                        if not windowed:
                            ins = nc.vector.scalar_tensor_tensor(move[:, :], count[:, :], 1.0, away[:, :],
                                                                 ALU.min, ALU.mult)
                        ins.then_inc(level, 1)
                        reached(3)
                        if not windowed:
                            tt(MV[:, :, :, 0:64], bc(qs[b][:, :, :], 2, 3), bc(e[:, :, :], 3, S_CH), ALU.mult)
                        tt(cross[:, :, 2:5:2, :], bc(y[:, :, 0, :], 2, 2), bc(e[:, :, 1:3], 3, V_CH), ALU.mult)
                        tt(cross[:, :, 1:4:2, :], bc(y[:, :, 2, :], 2, 2), bc(e[:, :, 0:2], 3, V_CH), ALU.mult)
                        tt(cross[:, :, 0, :], y[:, :, 1, :], bc(e[:, :, 2], 2, V_CH), ALU.mult)
                        tt(cross[:, :, 5, :], y[:, :, 1, :], bc(e[:, :, 0], 2, V_CH), ALU.mult)
                        tt(dd[:, :, :], d[:, :, 0, :], d[:, :, 1, :], ALU.add).then_inc(level, 1)
                        reached(4)
                        tt(dd[:, :, :], dd[:, :, :], d[:, :, 2, :], ALU.add).then_inc(level, 1)
                        tt(MV[:, :, :, 96:128], cross[:, :, 0:3, :], cross[:, :, 3:6, :], ALU.subtract)
                        reached(5)
                        ins = tt(M[:, :, 64:96], dd[:, :, :], W[:, :, W_DOT:W_CROSS], ALU.mult)
                        if not windowed:
                            for j in range(G):
                                wait(dve, added[b][j], i * 16)
                            ins = tt(slot[b][:, :], move[:, :], keys_c, ALU.add)
                        ins.then_inc(messages[b], 1)

                loop(dve, 0, LAST + 1, both)

            choose(dve, program)

_WEIGHTS = {
    0: {"skip_s": "L0_gnn_W_skip0", "skip_v": "L0_gnn_W_skip1", "lin_s": "L0_gnn_W_nl0",
        "lin_v": "L0_gnn_W_nl1", "fc1": "L0_gnn_W_fc1", "fc2": "L0_gnn_W_fc2",
        "out_s": "L0_gnn_W_out_s", "out_v": "L0_gnn_W_out_v"},
    1: {"skip_s": "L1_gnn_sc_ws", "skip_v": "L1_gnn_sc_wv", "lin_s": "L1_gnn_lin1_ws",
        "lin_v": "L1_gnn_lin1_wv", "fc1": "L1_gnn_fc_w1", "fc2": "L1_gnn_fc_w2",
        "out_s": "L1_gnn_lin2_ws", "out_v": "L1_gnn_lin2_wv"},
}


def build(nc, t, out):
    ctx = ExitStack()
    with ctx:
        k = allocate(nc, ctx)
        w = {l: {name: t[full] for name, full in _WEIGHTS[l].items()} for l in (0, 1)}
        setup_phase(nc, k, w, t["ea3"], t["attr"], t["dst_col"])
        node_phase(nc, k, 0, t["x"], None)
        edge_phase(nc, k, 0, t["ef"], t["dst_col"], t["src_col"], t["src_row"], k.rhat)
        node_phase(nc, k, 1, t["x"], k.x1)
        edge_phase(nc, k, 1, t["ef"], t["src_col"], t["dst_col"], t["dst_row"], t["e1"], t["e0"])
        node_phase(nc, k, 2, k.x1, out)


def kernel(**inputs):
    import concourse.bacc as bacc
    from concourse.bass_utils import run_bass_kernel_spmd

    a = {name: np.asarray(v) for name, v in inputs.items()}

    def by_component(x):
        v = x[:, S_CH:].reshape(-1, V_CH, 3).transpose(0, 2, 1).reshape(-1, 3 * V_CH)
        return np.concatenate([x[:, :S_CH], v], 1)

    def by_tile(e):
        return e.reshape(GROUPS, G, P, -1).transpose(2, 0, 1, 3)

    host = {
        "x": by_component(a["x"]).reshape(P, NT * CH),
        "ef": a["edge_attr_64"].reshape(GROUPS, 2, 4, P, HID).transpose(0, 1, 4, 2, 3).reshape(GROUPS * 128, 4 * P),
        "src_col": by_tile(a["src"]).reshape(P, -1),
        "dst_col": by_tile(a["dst"]).reshape(P, -1),
        "src_row": a["src"].reshape(GROUPS, G * P),
        "dst_row": a["dst"].reshape(GROUPS, G * P),
        "ea3": by_tile(a["edge_attr_3"]).reshape(P, -1),
        "e0": by_tile(a["edge_attr_4"][:, 0:1]).reshape(P, -1),
        "e1": by_tile(a["edge_attr_4"][:, 1:4]).reshape(P, -1),
        "attr": a["node_vec1"].reshape(P, NT),
    }
    for names in _WEIGHTS.values():
        host.update({name: a[name] for name in names.values()})
    nc = bacc.Bacc("TRN2", target_bir_lowering=False, num_devices=1)
    host = {name: np.ascontiguousarray(v) for name, v in host.items()}
    aps = {name: nc.dram_tensor(f"in_{name}", v.shape, mybir.dt.from_np(v.dtype), kind="ExternalInput").ap()
           for name, v in host.items()}
    out = nc.dram_tensor("out", [P, NT * CH], FP32, kind="ExternalOutput").ap()
    build(nc, aps, out)
    r = run_bass_kernel_spmd(nc, [{f"in_{name}": v for name, v in host.items()}], core_ids=[0])
    y = r.results[0]["out"].reshape(NODES, CH)
    v = y[:, S_CH:].reshape(NODES, 3, V_CH).transpose(0, 2, 1).reshape(NODES, 3 * V_CH)
    return np.concatenate([y[:, :S_CH], v], 1)
```

```python
import numpy as np
import concourse.bass as bass
from concourse import mybir
from contextlib import ExitStack

FP32 = mybir.dt.float32
INT32 = mybir.dt.int32
ALU = mybir.AluOpType
ACT = mybir.ActivationFunctionType
AX = mybir.AxisListType

P = 125
NODES = 6250
EDGES = 200000
S_CH, V_CH = 64, 32
CH = S_CH + 3 * V_CH
NT = NODES // P
NB = 5
STEPS = NT // NB
G = 8
GROUPS = EDGES // (P * G)
HID = 64
WCOLS = 224
MSG = 96 + 3 * 128
OUT = 96 + 3 * V_CH
FEATS = 352
ROW = 256
X_TILES = 3
ACCS = 4
ACC_ROWS = NODES + 2 * P
WINDOW = 128
ZERO_PARTS = 6
ZERO_COLS = ACC_ROWS // P * OUT // ZERO_PARTS
MAPS = CH + OUT
MAPS_A = MAPS - 2 * V_CH
BANK = 512
W_SS, W_VV, W_SV, W_DOT, W_CROSS = 0, 64, 96, 160, 192


def bc(ap, axis, n):
    ap = ap.unsqueeze(axis)
    shape = list(ap.shape)
    shape[axis] = n
    return ap.to_broadcast(shape)


def due(n, least=1):
    return not isinstance(n, int) or n >= least


def loop(engine, first, end, body, peel=1):
    for i in range(first, first + peel):
        body(i)
    with engine.Fori(first + peel, end) as i:
        body(i)


def exists(i):
    return not isinstance(i, int) or i >= 0


class Phase:
    pass


def allocate(nc, ctx):
    k = Phase()

    def sb(name, shape, dt=FP32):
        return ctx.enter_context(nc.sbuf_tensor(name, shape, dt))

    k.zero = sb("zero", [P, ZERO_COLS])
    k.zeroed = [ctx.enter_context(nc.semaphore(f"zeroed{l}")) for l in (0, 1)]
    k.ident = sb("ident", [128, 128])
    k.earlier = sb("earlier", [P, P])
    k.trash_i = sb("trash_i", [P, 1], INT32)
    k.trash = sb("trash", [P, 1])
    k.attr_c = sb("attr_c", [P, NT])
    k.iota_row = sb("iota_row", [P, WINDOW])
    k.base = sb("base", [128, GROUPS])
    k.rows = sb("rows", [128, GROUPS], INT32)
    k.rows_f = sb("rows_f", [128, GROUPS])
    k.near = sb("near", [128, GROUPS], INT32)
    k.narrow = sb("narrow", [128, 1], INT32)
    k.maps_a = [sb(f"maps_a{l}", [128, MAPS_A]) for l in (0, 1)]
    k.maps_b = [sb(f"maps_b{l}", [V_CH, 2 * V_CH]) for l in (0, 1)]
    k.fc1 = [sb(f"fc1_{l}", [128, 128]) for l in (0, 1)]
    k.fc2 = [sb(f"fc2_{l}", [128, WCOLS]) for l in (0, 1)]
    k.out_s = [sb(f"out_s{l}", [96, 96]) for l in (0, 1)]
    k.out_v = [sb(f"out_v{l}", [128, V_CH]) for l in (0, 1)]
    k.map_q = [sb(f"map_q{l}", [128, 64]) for l in (0, 1)]
    k.map_yz = [sb(f"map_yz{l}", [128, 64]) for l in (0, 1)]
    k.banks = [ctx.enter_context(nc.psum_tensor(f"bank{n}", [128, BANK], FP32)) for n in range(8)]
    k.table = [nc.dram_tensor(f"table{l}", [NODES, CH], FP32).ap() for l in (0, 1)]
    k.x1 = nc.dram_tensor("x1", [P, NT * CH], FP32).ap()
    k.spans = nc.dram_tensor("spans", [GROUPS // 2, 4], FP32).ap()
    k.rhat = nc.dram_tensor("rhat", [P, GROUPS * G * 3], FP32).ap()
    k.acc = [[nc.dram_tensor(f"acc{l}_{n}", [ACC_ROWS, OUT], FP32).ap() for n in range(ACCS)]
             for l in (0, 1)]
    return k


def zero_part(engine, k, layer, n, m):
    view = k.acc[layer][n].rearrange("(p t) c -> p (t c)", p=P)
    engine.dma_start(view[:, m * ZERO_COLS:(m + 1) * ZERO_COLS], k.zero[:, :]).then_inc(k.zeroed[layer], 16)


def zero_past_nodes(engine, k, layer):
    rows = k.acc[layer][0][NODES:ACC_ROWS, :].rearrange("(p t) c -> p (t c)", p=P)
    engine.dma_start(rows, k.zero[:, 0:2 * OUT]).then_inc(k.zeroed[layer], 16)


ZEROINGS = (ACCS - 1) * ZERO_PARTS + 1


def setup_phase(nc, k, w, ea3, attr, dst_col):
    ctx = ExitStack()
    with ctx:
        def sb(name, shape, dt=FP32):
            return ctx.enter_context(nc.sbuf_tensor(name, shape, dt))

        def sem(name):
            return ctx.enter_context(nc.semaphore(name))

        CHUNKS = 4
        EC = GROUPS * G // CHUNKS
        ea = sb("ea", [P, CHUNKS, EC * 3])
        sq = sb("sq", [P, EC * 3])
        ss = sb("ss", [P, EC])
        nrm = sb("nrm", [P, EC])
        inv = sb("inv", [P, EC])
        HALF = GROUPS // 2
        dst = sb("dst", [P, GROUPS, G], INT32)
        ends_p = sb("ends_p", [P, 4, HALF])
        ends = sb("ends", [HALF, 4])
        ends_row = sb("ends_row", [128, HALF, 4])
        span = sb("span", [128, GROUPS])
        widest = sb("widest", [128, 1])
        iota_ri = sb("iota_ri", [P, WINDOW], INT32)
        iota_pi = sb("iota_pi", [128, 1], INT32)
        iota_p = sb("iota_p", [128, 1])

        s_cleared, s_weights, s_attr = sem("cleared"), sem("weights"), sem("attr")
        s_ea = [sem(f"ea_in{c}") for c in range(CHUNKS)]
        s_sum, s_norm, s_step, s_unit, s_stored = (
            sem("sum_sq"), sem("norm"), sem("dve_step"), sem("unit"), sem("rhat_stored"))
        s_filled, s_mask = sem("filled"), sem("masks")
        s_dst, s_ends_p, s_ends_ps, s_ends, s_spans, s_row, s_last = (
            sem("dst_in"), sem("ends_p"), sem("ends_psum"), sem("ends"), sem("spans_out"), sem("ends_row"),
            sem("last"))
        block = ctx.enter_context(nc.Block())

        @block.sync
        def _(sp):
            sp.dma_start(dst[:, :, :].rearrange("p g j -> p (g j)"), dst_col).then_inc(s_dst, 16)
            for c in range(CHUNKS):
                sp.dma_start(ea[:, c, :], ea3[:, c * EC * 3:(c + 1) * EC * 3]).then_inc(s_ea[c], 16)
            sp.dma_start(k.attr_c[:, :], attr).then_inc(s_attr, 16)
            sp.wait_ge(s_cleared, 1)
            n = 0
            for l in (0, 1):
                a, b, fc1, fc2 = k.maps_a[l], k.maps_b[l], k.fc1[l], k.fc2[l]
                t0 = 128 + 96
                for to, of in (
                    (a[0:64, 0:64], w[l]["lin_s"]), (a[0:64, 128:224], w[l]["skip_s"]),
                    (a[64:96, 64:96], w[l]["lin_v"]), (a[96:128, 96:128], w[l]["lin_v"]),
                    (b[:, 0:32], w[l]["lin_v"]),
                    (a[64:96, t0:t0 + 32], w[l]["skip_v"]), (a[96:128, t0 + 32:t0 + 64], w[l]["skip_v"]),
                    (b[:, 32:64], w[l]["skip_v"]),
                    (fc1[0:64, 0:64], w[l]["fc1"]), (fc1[64:128, 64:128], w[l]["fc1"]),
                    (k.out_s[l][:, :], w[l]["out_s"]),
                    (k.out_v[l][:, :], w[l]["out_v"]),
                    (k.map_q[l][0:64, 0:32], w[l]["out_v"][0:64, :]),
                    (k.map_q[l][64:128, 32:64], w[l]["out_v"][64:128, :]),
                    (k.map_yz[l][0:64, 0:32], w[l]["out_v"][64:128, :]),
                    (k.map_yz[l][64:128, 32:64], w[l]["out_v"][64:128, :]),
                ):
                    sp.dma_start(to, of).then_inc(s_weights, 16)
                    n += 1
                for half in (0, 64):
                    for to, of, size in ((W_SS, 0, 64), (W_SV, 64, 64), (W_VV, 128, 32),
                                         (W_DOT, 160, 32), (W_CROSS, 192, 32)):
                        sp.dma_start(fc2[half:half + 64, to:to + size],
                                     w[l]["fc2"][:, of:of + size]).then_inc(s_weights, 16)
                        n += 1
            sp.wait_ge(s_ends, 4)
            sp.dma_start(k.spans, ends[:, :]).then_inc(s_spans, 16)
            sp.wait_ge(s_spans, 16)
            sp.dma_start(ends_row[:, :, :].rearrange("p g e -> p (g e)"),
                         k.spans.rearrange("(o g) e -> o (g e)", o=1).to_broadcast([128, 2 * GROUPS])
                         ).then_inc(s_row, 16)
            for c in range(CHUNKS):
                sp.wait_ge(s_unit, c + 1)
                sp.dma_start(k.rhat[:, c * EC * 3:(c + 1) * EC * 3], ea[:, c, :]).then_inc(s_stored, 16)
            sp.wait_ge(s_stored, 16 * CHUNKS)
            sp.wait_ge(s_weights, 16 * n)
            sp.wait_ge(s_attr, 16)

        n_weights = 2 * (16 + 10)

        @block.gpsimd
        def _(pool):
            pool.iota(k.trash_i[:, :], pattern=[[0, 1]], base=NODES, channel_multiplier=1).then_inc(s_mask, 1)
            pool.iota(iota_ri[:, :], pattern=[[1, WINDOW]], base=0, channel_multiplier=0).then_inc(s_mask, 1)
            pool.iota(iota_pi[:, :], pattern=[[0, 1]], base=0, channel_multiplier=1).then_inc(s_mask, 1)
            pool.memset(k.ident[:, :], 0.0).then_inc(s_filled, 1)
            pool.memset(k.earlier[:, :], 1.0).then_inc(s_filled, 1)
            pool.wait_ge(s_filled, 2)
            pool.affine_select(out=k.ident[:, :], in_=k.ident[:, :], compare_op=ALU.not_equal, fill=1.0,
                               base=0, pattern=[[-1, 128]], channel_multiplier=1).then_inc(s_mask, 1)
            pool.affine_select(out=k.earlier[:, :], in_=k.earlier[:, :], compare_op=ALU.is_gt, fill=0.0,
                               base=0, pattern=[[-1, P]], channel_multiplier=1).then_inc(s_mask, 1)
            pool.wait_ge(s_mask, 5)

        @block.scalar
        def _(act):
            for c in range(CHUNKS):
                act.wait_ge(s_sum, c + 1)
                if c:
                    act.wait_ge(s_unit, c)
                nc.scalar.activation(nrm[:, :], ss[:, :], ACT.Sqrt).then_inc(s_norm, 1)

        @block.tensor
        def _(pe):
            pe.wait_ge(s_mask, 5)
            pe.wait_ge(s_ends_p, 4)
            for c in range(4):
                nc.tensor.transpose(k.banks[c][0:HALF, 0:P], ends_p[:, c, :], k.ident[0:P, 0:P]).then_inc(s_ends_ps, 1)

        @block.vector
        def _(dve):
            nc.vector.memset(k.zero[:, :], 0.0)
            dve.wait_ge(s_dst, 16)
            for c in range(4):
                lo = HALF * (c % 2)
                nc.vector.tensor_reduce(ends_p[:, c, :], dst[:, lo:lo + HALF, :], AX.X,
                                        ALU.min if c < 2 else ALU.max).then_inc(s_ends_p, 1)
            for l in (0, 1):
                for weights in (k.maps_a[l], k.maps_b[l], k.fc1[l], k.map_q[l], k.map_yz[l]):
                    last = nc.vector.memset(weights[:, :], 0.0)
            last.then_inc(s_cleared, 1)
            steps = 0
            for c in range(CHUNKS):
                v = ea[:, c, :].rearrange("p (e i) -> p e i", i=3)
                dve.wait_ge(s_ea[c], 16)
                nc.vector.tensor_tensor(sq[:, :], ea[:, c, :], ea[:, c, :], ALU.mult).then_inc(s_step, 1)
                dve.wait_ge(s_step, 2 * c + 1)
                nc.vector.tensor_reduce(ss[:, :], sq[:, :].rearrange("p (e i) -> p e i", i=3), AX.X,
                                        ALU.add).then_inc(s_sum, 1)
                dve.wait_ge(s_norm, c + 1)
                nc.vector.reciprocal(inv[:, :], nrm[:, :]).then_inc(s_step, 1)
                dve.wait_ge(s_step, 2 * c + 2)
                nc.vector.tensor_tensor(v, v, bc(inv[:, :], 2, 3), ALU.mult).then_inc(s_unit, 1)
            dve.wait_ge(s_mask, 5)
            nc.vector.tensor_copy(k.trash[:, :], k.trash_i[:, :])
            nc.vector.tensor_copy(k.iota_row[:, :], iota_ri[:, :])
            nc.vector.tensor_copy(iota_p[:, :], iota_pi[:, :]).then_inc(s_last, 1)
            for c in range(4):
                dve.wait_ge(s_ends_ps, c + 1)
                nc.vector.tensor_reduce(ends[:, c:c + 1], k.banks[c][0:HALF, 0:P], AX.X,
                                        ALU.min if c < 2 else ALU.max).then_inc(s_ends, 1)
            dve.wait_ge(s_row, 16)
            dve.wait_ge(s_last, 1)
            by_half = ends_row[:, :, :].rearrange("p g e -> p e g")
            least, greatest = by_half[:, 0:2, :], by_half[:, 2:4, :]

            def halves(x):
                return x[:, :].rearrange("p (h g) -> p h g", h=2)

            nc.vector.tensor_copy(halves(k.base), least)
            nc.vector.tensor_scalar(halves(k.rows), least, iota_p[:, 0:1], None, ALU.add)
            nc.vector.tensor_scalar(halves(k.rows_f), least, iota_p[:, 0:1], None, ALU.add)
            nc.vector.tensor_scalar(halves(k.near), least, iota_p[:, 0:1], float(NODES - 1), ALU.add, ALU.min)
            nc.vector.tensor_tensor(halves(span), greatest, least,
                                    ALU.subtract).then_inc(s_last, 1)
            dve.wait_ge(s_last, 2)
            nc.vector.tensor_reduce(widest[:, :], span[:, :], AX.X, ALU.max).then_inc(s_last, 1)
            dve.wait_ge(s_last, 3)
            nc.vector.tensor_scalar(k.narrow[:, :], widest[:, :], float(WINDOW), None, ALU.is_lt)
            dve.wait_ge(s_weights, 16 * n_weights)
            r2, r3 = 2.0 ** -0.5, 3.0 ** -0.5
            common1 = (1.0 / HID ** 0.5) * 16.0 ** -0.5
            cs, cv = common1 * 96.0 ** -0.5, common1 * 128.0 ** -0.5
            f0, f1 = (3.0 ** 0.5 / 32, 1 / 32.0, 3.0 ** 0.5 * r2 / 32), (cv, cv, cv * r2)
            for weights, lo, hi, factor in (
                (k.map_q[0], 0, 64, f0[0]), (k.map_q[0], 64, 96, f0[1]), (k.map_q[0], 96, 128, f0[2]),
                (k.map_q[1], 0, 64, f1[0]), (k.map_q[1], 64, 96, f1[1]), (k.map_q[1], 96, 128, f1[2]),
                (k.map_yz[0], 0, 32, f0[1]), (k.map_yz[0], 32, 64, f0[2]),
                (k.map_yz[0], 64, 96, f0[1]), (k.map_yz[0], 96, 128, f0[2]),
                (k.map_yz[1], 0, 32, f1[1]), (k.map_yz[1], 32, 64, f1[2]),
                (k.map_yz[1], 64, 96, f1[1]), (k.map_yz[1], 96, 128, f1[2]),
                (k.out_s[0], 0, 96, 1 / 32.0),
                (k.out_v[0], 0, 64, f0[0]), (k.out_v[0], 64, 96, f0[1]), (k.out_v[0], 96, 128, f0[2]),
                (k.maps_a[1], 0, 64, S_CH ** -0.5), (k.maps_a[1], 64, 128, V_CH ** -0.5),
                (k.maps_b[1], 0, 32, V_CH ** -0.5),
                (k.out_s[1], 0, 64, cs), (k.out_s[1], 64, 96, cs * r3),
                (k.out_v[1], 0, 64, f1[0]), (k.out_v[1], 64, 96, f1[1]), (k.out_v[1], 96, 128, f1[2]),
            ):
                part = weights[lo:hi, :]
                nc.vector.tensor_scalar(part, part, factor, None, ALU.mult)


def node_phase(nc, k, phase, x_in, x_out):
    combine, project = phase > 0, phase < 2
    ctx = ExitStack()
    with ctx:
        def sb(name, shape, dt=FP32):
            return ctx.enter_context(nc.sbuf_tensor(f"nodes{phase}_{name}", shape, dt))

        def sem(name):
            return ctx.enter_context(nc.semaphore(f"n{phase}_{name}"))

        x = [sb(f"x{b}", [P, NB, CH]) for b in (0, 1)]
        if combine:
            acc = [sb(f"acc{b}", [P, ACCS, NB, OUT]) for b in (0, 1)]
            gate = sb("gate", [P, NB, 96])
            y = sb("y", [P, NB, CH])
            x1 = sb("sum", [P, NB, CH])
        if project:
            cent = sb("cent", [P, NB, CH])
            square = sb("square", [P, NB, CH])
            sum_x, mean, sum_sq, var, std, rstd = (
                sb(name, [P, NB]) for name in ("sum_x", "mean", "sum_sq", "var", "std", "rstd"))
            h = sb("h", [P, NB, CH])
            hT_a = sb("hT_a", [128, NB, P])
            hT_b = sb("hT_b", [V_CH, NB, P])
            maps = sb("maps", [P, NB, MAPS])
            maps_a, maps_b = k.maps_a[phase], k.maps_b[phase]
        in_dma = [sem(f"in_dma{b}") for b in (0, 1)]
        dve_done = sem("dve_done")
        if combine:
            gated, x1_stored = sem("gated"), sem("x1_stored")
        if project:
            std_ready, table_stored, skip_stored = sem("std_ready"), sem("table_stored"), sem("skip_stored")
            transposed, hT_ready, mapped, maps_ready = (
                sem("transposed"), sem("hT_ready"), sem("mapped"), sem("maps_ready"))
        last = phase - 1

        order = (["pairs", "pre", "scaled", "scalars", "vectors", "x1"] if combine else []) + (
            ["sum_x", "mean", "cent", "square", "sum_sq", "var", "rstd", "h"] if project else [])
        if phase == 1:
            order.remove("scaled")

        def upto(n, name):
            return n * len(order) + (order.index(name) + 1)

        PRE = "scaled" if phase == 2 else "pre"
        IN_USED = "x1" if combine else "cent"
        block = ctx.enter_context(nc.Block())

        def choose(engine, program):
            if phase < 2:
                program(ACCS if combine else 0)
                return
            narrow = engine.value_load(k.narrow[0:1, 0:1], min_val=0, max_val=1)
            with engine.If(narrow):
                program(2)
            with engine.Else():
                program(ACCS)

        @block.sync
        def _(sp):
            def program(copies):
                def load(n, b):
                    sp.dma_start(x[b][:, :, :].rearrange("p t c -> p (t c)"),
                                 x_in[:, bass.ds(n * (NB * CH), NB * CH)]).then_inc(in_dma[b], 16)
                    for a in range(copies):
                        sums = k.acc[last][a][0:NODES, :].rearrange("(p t) c -> p (t c)", p=P)
                        sp.dma_start(acc[b][:, a, :, :].rearrange("p t c -> p (t c)"),
                                     sums[:, bass.ds(n * (NB * OUT), NB * OUT)]).then_inc(in_dma[b], 16)

                load(0, 0)
                load(1, 1)
                with sp.Fori(1, STEPS // 2) as i:
                    for b in (0, 1):
                        sp.wait_ge(dve_done, upto(i * 2 + (b - 2), IN_USED))
                        load(i * 2 + b, b)

            choose(sp, program)
            if phase == 0:
                zero_past_nodes(sp, k, 0)
                for m in range(ZERO_PARTS):
                    zero_part(sp, k, 0, 1, m)
            if phase == 1:
                sp.wait_ge(k.zeroed[1], 16 * ZEROINGS)

        @block.vector
        def _(dve):
            def program(copies):
                def both(i):
                    for b in (0, 1):
                        n = i * 2 + b
                        src = x1 if combine else x[b]
                        dve.wait_ge(in_dma[b], (i + 1) * (16 * (1 + copies)))
                        if combine:
                            A, pre = acc[b], acc[b][:, 0, :, :]
                            if copies == 4:
                                nc.vector.tensor_tensor(A[:, 0:2, :, :].rearrange("p a t c -> p (a t c)"),
                                                        A[:, 0:2, :, :].rearrange("p a t c -> p (a t c)"),
                                                        A[:, 2:4, :, :].rearrange("p a t c -> p (a t c)"),
                                                        ALU.add).then_inc(dve_done, 1)
                                dve.wait_ge(dve_done, upto(n, "pairs"))
                            nc.vector.tensor_tensor(pre, pre, A[:, 1, :, :], ALU.add
                                                    ).then_inc(dve_done, 1 if copies == 4 else 2)
                            dve.wait_ge(dve_done, upto(n, "pre"))
                            if phase == 2:
                                nc.vector.tensor_tensor(
                                    pre, pre, bc(k.attr_c[:, bass.ds(n * NB, NB)], 2, OUT),
                                    ALU.mult).then_inc(dve_done, 1)
                            dve.wait_ge(gated, n + 1)
                            nc.vector.tensor_tensor(y[:, :, 0:S_CH], pre[:, :, 0:S_CH], gate[:, :, 0:S_CH],
                                                    ALU.mult).then_inc(dve_done, 1)
                            for c in range(3):
                                lo = S_CH + V_CH * c
                                ins = nc.vector.tensor_tensor(
                                    y[:, :, lo:lo + V_CH], pre[:, :, 96 + V_CH * c:96 + V_CH * (c + 1)],
                                    gate[:, :, S_CH:96], ALU.mult)
                            ins.then_inc(dve_done, 1)
                            dve.wait_ge(dve_done, upto(n, "vectors"))
                            if due(n):
                                dve.wait_ge(x1_stored, n * 16)
                            nc.vector.tensor_tensor(x1[:, :, :], x[b][:, :, :], y[:, :, :],
                                                    ALU.add).then_inc(dve_done, 1)
                            dve.wait_ge(dve_done, upto(n, "x1"))
                        if project:
                            nc.vector.tensor_reduce(sum_x[:, :], src[:, :, :], AX.X, ALU.add).then_inc(dve_done, 1)
                            dve.wait_ge(dve_done, upto(n, "sum_x"))
                            nc.vector.tensor_scalar(mean[:, :], sum_x[:, :], 1.0 / CH, None,
                                                    ALU.mult).then_inc(dve_done, 1)
                            dve.wait_ge(dve_done, upto(n, "mean"))
                            nc.vector.tensor_tensor(cent[:, :, :], src[:, :, :], bc(mean[:, :], 2, CH),
                                                    ALU.subtract).then_inc(dve_done, 1)
                            dve.wait_ge(dve_done, upto(n, "cent"))
                            nc.vector.tensor_tensor(square[:, :, :], cent[:, :, :], cent[:, :, :],
                                                    ALU.mult).then_inc(dve_done, 1)
                            dve.wait_ge(dve_done, upto(n, "square"))
                            nc.vector.tensor_reduce(sum_sq[:, :], square[:, :, :], AX.X, ALU.add).then_inc(dve_done, 1)
                            dve.wait_ge(dve_done, upto(n, "sum_sq"))
                            nc.vector.tensor_scalar(var[:, :], sum_sq[:, :], 1.0 / CH, 1e-5, ALU.mult,
                                                    ALU.add).then_inc(dve_done, 1)
                            dve.wait_ge(std_ready, n + 1)
                            nc.vector.reciprocal(rstd[:, :], std[:, :]).then_inc(dve_done, 1)
                            dve.wait_ge(dve_done, upto(n, "rstd"))
                            if due(n):
                                dve.wait_ge(transposed, n)
                            nc.vector.scalar_tensor_tensor(h[:, :, :], cent[:, :, :], 0.0, bc(rstd[:, :], 2, CH),
                                                           ALU.max, ALU.mult).then_inc(dve_done, 1)

                loop(dve, 0, STEPS // 2, both)

            choose(dve, program)

        @block.scalar
        def _(act):
            def transposed_out(n):
                act.wait_ge(transposed, n + 1)
                for to, of, rows in ((hT_a, 0, 128), (hT_b, 2, V_CH)):
                    nc.scalar.activation(
                        to[:, 0:4, :].rearrange("r t p -> r (t p)"),
                        k.banks[of][0:rows, 0:4 * P], ACT.Copy).then_inc(hT_ready, 1)
                nc.scalar.activation(hT_a[:, 4, :], k.banks[1][:, 0:P], ACT.Copy).then_inc(hT_ready, 1)
                nc.scalar.activation(hT_b[:, 4, :], k.banks[1][0:V_CH, P:2 * P],
                                     ACT.Copy).then_inc(hT_ready, 1)

            def maps_out(n):
                if due(n):
                    act.wait_ge(table_stored, n * 16)
                if due(n):
                    act.wait_ge(skip_stored, n * 16)
                for t in range(NB):
                    act.wait_ge(mapped, n * NB + (t + 1))
                    bank = k.banks[3 + t]
                    blocks = maps[:, t, :].rearrange("p (h c) -> p h c", c=V_CH)
                    nc.scalar.activation(maps[:, t, CH:MAPS - V_CH], bank[0:P, 128:MAPS_A], ACT.Copy)
                    if phase == 1:
                        by_node = k.attr_c[:, bass.ds(n * NB + t, 1)]
                        nc.scalar.activation(maps[:, t, 0:128], bank[0:P, 0:128], ACT.Copy, scale=by_node)
                        nc.scalar.activation(maps[:, t, 128:CH], bank[0:P, MAPS_A:MAPS_A + V_CH], ACT.Copy,
                                             scale=by_node)
                        nc.scalar.activation(maps[:, t, MAPS - V_CH:MAPS], bank[0:P, MAPS_A + V_CH:MAPS],
                                             ACT.Copy).then_inc(maps_ready, 1)
                    else:
                        nc.scalar.activation(maps[:, t, 0:128], bank[0:P, 0:128], ACT.Copy)
                        nc.scalar.activation(blocks[:, 4:11:6, :],
                                             bank[0:P, MAPS_A:MAPS].rearrange("p (h c) -> p h c", c=V_CH),
                                             ACT.Copy).then_inc(maps_ready, 1)
                act.wait_ge(maps_ready, (n + 1) * NB)
                rows = k.table[phase].rearrange("(p t) c -> p t c", p=P)
                act.dma_start(rows[:, bass.ds(n * NB, NB), :], maps[:, :, 0:CH]).then_inc(table_stored, 16)
                rows = k.acc[phase][0][0:NODES, :].rearrange("(p t) c -> p t c", p=P)
                act.dma_start(rows[:, bass.ds(n * NB, NB), :], maps[:, :, CH:MAPS]).then_inc(skip_stored, 16)

            def both(i):
                for b in (0, 1):
                    n = i * 2 + b
                    has_before = project and exists(n - 1)
                    if combine:
                        act.wait_ge(dve_done, upto(n, PRE))
                        nc.scalar.activation(gate[:, :, :], acc[b][:, 0, :, 0:96], ACT.Sigmoid).then_inc(gated, 1)
                    if has_before:
                        transposed_out(n - 1)
                    if combine:
                        act.wait_ge(dve_done, upto(n, "x1"))
                        act.dma_start(x_out[:, bass.ds(n * (NB * CH), NB * CH)],
                                      x1[:, :, :].rearrange("p t c -> p (t c)")).then_inc(x1_stored, 16)
                    if project:
                        act.wait_ge(dve_done, upto(n, "var"))
                        nc.scalar.activation(std[:, :], var[:, :], ACT.Sqrt).then_inc(std_ready, 1)
                    if has_before:
                        maps_out(n - 1)

            loop(act, 0, STEPS // 2, both)
            if project:
                transposed_out(STEPS - 1)
                maps_out(STEPS - 1)
            if combine:
                act.wait_ge(x1_stored, STEPS * 16)
            if project:
                act.wait_ge(table_stored, STEPS * 16)
                act.wait_ge(skip_stored, STEPS * 16)

        if project:
            @block.tensor
            def _(pe):
                def step(n):
                    pe.wait_ge(dve_done, upto(n, "h"))
                    if due(n):
                        pe.wait_ge(hT_ready, n * 4)
                    for t in range(NB):
                        bank, col = (0, t * P) if t < 4 else (1, 0)
                        nc.tensor.transpose(k.banks[bank][:, col:col + P], h[:, t, 0:128], k.ident[0:P, 0:P])
                        bank, col = (2, t * P) if t < 4 else (1, P)
                        ins = nc.tensor.transpose(k.banks[bank][0:V_CH, col:col + P], h[:, t, 128:CH],
                                                  k.ident[0:P, 0:P])
                    ins.then_inc(transposed, 1)
                    pe.wait_ge(hT_ready, (n + 1) * 4)
                    if due(n):
                        pe.wait_ge(maps_ready, n * NB)
                    for t in range(NB):
                        bank = k.banks[3 + t]
                        nc.tensor.matmul(bank[0:P, 0:MAPS_A], hT_a[:, t, :], maps_a[:, :], start=True, stop=True)
                        nc.tensor.matmul(bank[0:P, MAPS_A:MAPS], hT_b[:, t, :], maps_b[:, :], start=True,
                                         stop=True).then_inc(mapped, 1)

                loop(pe, 0, STEPS, step)


def edge_phase(nc, k, layer, ef, idx, idx_rows, keycol, keys, vec, e0=None):
    ctx = ExitStack()
    with ctx:
        def sb(name, shape, dt=FP32):
            return ctx.enter_context(nc.sbuf_tensor(f"e{layer}_{name}", shape, dt))

        def two(name, shape, dt=FP32):
            return [sb(f"{name}{b}", shape, dt) for b in (0, 1)]

        def sem(name):
            return ctx.enter_context(nc.semaphore(f"e{layer}_{name}"))

        def sems(name, n=2):
            return [sem(f"{name}{m}") for m in range(n)]

        ef_in = two("ef", [128, 4 * P])
        idx_in = two("idx", [P, G], INT32)
        key_in = two("key", [P, G], INT32)
        keyrow = two("keyrow", [P, G, P], INT32)
        vec_in = two("vec", [P, G, 3])
        hid = two("hid", [128, 4 * P])
        wts = two("wts", [P, G, WCOLS])
        xg = two("xg", [P, G, CH])
        msg = two("msg", [P, G, MSG])
        same_in = two("same", [P, G, WINDOW])
        slot = two("slot", [P, G], INT32)
        outs = two("outs", [P, G, OUT])
        if layer == 1:
            e0_all = sb("e0_all", [P, GROUPS * G])
        qs = two("q", [P, G, S_CH])
        y = sb("y", [P, G, 3, V_CH])
        d = sb("d", [P, G, 3, V_CH])
        dd = sb("dd", [P, G, V_CH])
        cross = sb("cross", [P, G, 6, V_CH])
        masked = sb("masked", [P, G, P])
        count = sb("count", [P, G])
        away = sb("away", [P, G])
        move = sb("move", [P, G])
        target = sb("target", [P, G], INT32)
        turned = two("turned", [128, 3, P])
        mapped = two("mapped", [P, G, ROW])
        kept = two("kept", [P, G, 3])
        by_e = sb("by_e", [P, G, 3, V_CH])
        if layer == 0:
            hot = two("hot", [WINDOW, X_TILES * P])
            xw = two("xw", [WINDOW, CH])
            row_of = two("row_of", [WINDOW, X_TILES * P], INT32)
        fc1, fc2 = k.fc1[layer], k.fc2[layer]
        out_s, out_v = k.out_s[layer], k.out_v[layer]

        same = [x[:, :, :].rearrange("p g e -> p (g e)")[:, 0:G * P].rearrange("p (g e) -> p g e", e=P)
                for x in same_in]
        agg_sb = two("agg_sb", [128, MSG])
        winT = two("winT", [128, 4, WINDOW])
        win_outs = two("win_outs", [WINDOW, OUT])
        row_in = two("row_in", [WINDOW, 1], INT32)
        relative = sb("relative", [P, G])
        hid_ps = k.banks[0]
        w_ps, turned_ps, mapped_ps, sums_ps, x_ps = k.banks[1:3], k.banks[3:5], k.banks[5], k.banks[6], k.banks[7]
        agg_ps = k.banks[3:5]
        win_T_ps, win_out_ps = k.banks[5], k.banks[6]

        indexed, features, loaded, gathered = sems("indexed"), sems("features"), sems("loaded"), sems("gathered")
        keyed = sems("keyed")
        hid_psum, hid_ready = sems("hid_psum"), sems("hid_ready")
        messages = sems("messages")
        w_psum, w_ready = sems("w_psum"), sems("w_ready")
        slotted, finished = sem("slotted"), sem("finished")
        turned_psum, turned_ready = sem("turned_psum"), sem("turned_ready")
        mapped_psum, mapped_ready = sem("mapped_psum"), sem("mapped_ready")
        sums_psum, sums_ready = sem("sums_psum"), sem("sums_ready")
        if layer == 0:
            hot_ready, near_ready = sem("hot_ready"), sem("near_ready")
            x_psum, x_ready = sem("x_psum"), sem("x_ready")
            rows_in, window_in = sems("rows_in"), sems("window_in")
        added = [sems(f"added{b}_", G) for b in (0, 1)]
        passed = sem("passed")
        win_added = [added[0][0], added[1][0]]
        win_agg = [added[0][1], added[1][1]]
        win_rows = [added[0][2], added[1][2]]
        summed = [added[0][3], added[1][3]]
        q_ready, spread = slotted, finished
        if layer == 1:
            e0_in = sem("e0_in")
        level, side_level = sem("level"), sem("side_level")
        LAST = GROUPS // 2 - 1
        block = ctx.enter_context(nc.Block())

        def choose(engine, program):
            narrow = engine.value_load(k.narrow[0:1, 0:1], min_val=0, max_val=1)
            with engine.If(narrow):
                program(layer == 0, layer == 1)
            with engine.Else():
                program(False, False)

        def nth(i, b, q):
            return i * 4 + (2 * b + q // 2)

        def pair(i, b, q):
            return i * 8 + (4 * b + q)

        def before(i, b):
            return (i, 0) if b else (i - 1, 1)

        @block.sync
        def _(sp):
            def program(x_window, windowed):
                gathers = G - X_TILES if x_window else G

                def load_early(i, b):
                    g = i * 2 + b
                    if due(i):
                        sp.wait_ge(gathered[b], i * (16 * gathers))
                    sp.dma_start(idx_in[b][:, :], idx[:, bass.ds(g * G, G)]).then_inc(indexed[b], 16)
                    if due(i):
                        sp.wait_ge(hid_psum[b], i)
                    sp.dma_start(ef_in[b][:, :], ef[bass.ds(g * 128, 128), :]).then_inc(features[b], 16)

                def load_vectors(i, b):
                    g = i * 2 + b
                    if windowed:
                        if due(i):
                            sp.wait_ge(messages[b], i)
                        sp.dma_start(key_in[b][:, :], keycol[:, bass.ds(g * G, G)]).then_inc(keyed[b], 16)
                        if due(i):
                            sp.wait_ge(spread, i * 2 + (b - 1))
                    else:
                        first = isinstance(i, int) and (i, b) == (1, 0)
                        if due(i):
                            sp.wait_ge(slotted, 1 if first else i * 2 + (b - 2))
                    sp.dma_start(vec_in[b][:, :, :].rearrange("p g a -> p (g a)"),
                                 vec[:, bass.ds(g * (G * 3), G * 3)]).then_inc(loaded[b], 16)

                def load_keys(i, b):
                    g, b = i * 2 + (b - 1), 1 - b
                    col = keycol[:, bass.ds(g * G, G)]
                    row = keys[bass.ds(g, 1), :].to_broadcast([P, G * P])
                    if due(g, 2):
                        sp.wait_ge(slotted, g - 1)
                    sp.dma_start(keyrow[b][:, :, :].rearrange("p g e -> p (g e)"), row).then_inc(keyed[b], 16)
                    sp.dma_start(key_in[b][:, :], col).then_inc(keyed[b], 16)

                def load_rows(i, b):
                    if x_window:
                        if due(i):
                            sp.wait_ge(hot_ready, i * 2 + (b - 1))
                        sp.dma_start(row_of[b][:, :],
                                     idx_rows[bass.ds(i * 2 + b, 1), 0:X_TILES * P].to_broadcast(
                                         [WINDOW, X_TILES * P])).then_inc(rows_in[b], 16)

                def both(i, last=False):
                    part = i - 2 if layer == 0 and isinstance(i, int) else None
                    for b in (0, 1):
                        if part in range(ZERO_PARTS):
                            for copy in ((1,), (2, 3))[b]:
                                zero_part(sp, k, 1, copy, part)
                        if not (last and b):
                            load_early(*((i + 1, 0) if b else (i, 1)))
                        load_vectors(i, b)
                        if not last:
                            load_rows(i + 1, b)
                        if not windowed and exists(before(i, b)[0]):
                            load_keys(i, b)

                if layer == 0:
                    zero_past_nodes(sp, k, 1)
                load_rows(0, 0)
                load_rows(0, 1)
                load_early(0, 0)
                if layer == 1:
                    sp.dma_start(e0_all[:, :], e0).then_inc(e0_in, 16)
                loop(sp, 0, LAST, both, peel=2 + ZERO_PARTS if layer == 0 else 2)
                both(LAST, last=True)
                if not windowed:
                    load_keys(LAST + 1, 0)

            choose(sp, program)

        @block.gpsimd
        def _(pool):
            def program(x_window, windowed):
                def gather(i, b, j):
                    pool.indirect_dma_start(xg[b][:, j, :], None, k.table[layer],
                                            bass.IndirectOffsetOnAxis(ap=idx_in[b][:, j:j + 1], axis=0)
                                            ).then_inc(gathered[b], 16)

                def before_gathers(i, b):
                    pool.wait_ge(indexed[b], (i + 1) * 16)
                    if due(i):
                        pool.wait_ge(messages[b], i)
                    pool.sem_inc(passed, 1)

                def scatter(i, b, j):
                    if layer == 0 and isinstance(i, int) and i + b + j == 0:
                        pool.wait_ge(k.zeroed[0], 16 * ZEROINGS)
                    if j % 2 == 0:
                        pool.wait_ge(sums_ready, pair(i, b, j // 2) + 1)
                    if j >= ACCS:
                        pool.wait_ge(added[b][j - ACCS], (i + 1) * 16)
                    elif b:
                        pool.wait_ge(added[0][j + G - ACCS], (i + 1) * 16)
                    else:
                        if due(i):
                            pool.wait_ge(added[1][j + G - ACCS], i * 16)
                    pool.sem_inc(passed, 1)
                    pool.indirect_dma_start(k.acc[layer][j % ACCS],
                                            bass.IndirectOffsetOnAxis(ap=slot[b][:, j:j + 1], axis=0),
                                            outs[b][:, j, :], None, compute_op=ALU.add).then_inc(added[b][j], 16)

                def window(i, b):
                    n = i * 2 + b
                    if due(i):
                        pool.wait_ge(x_psum, i * 2 + (b - 1))
                    pool.sem_inc(passed, 1)
                    pool.tensor_copy(row_in[b][:, :], k.near[:, bass.ds(n, 1)]).then_inc(near_ready, 1)
                    pool.wait_ge(near_ready, n + 1)
                    pool.sem_inc(passed, 1)
                    pool.indirect_dma_start(xw[b][:, :], None, k.table[layer],
                                            bass.IndirectOffsetOnAxis(ap=row_in[b][:, 0:1], axis=0)
                                            ).then_inc(window_in[b], 16)

                def scatter_window(i, b):
                    pool.wait_ge(sums_ready, i * 2 + (b + 1))
                    if due(i):
                        pool.wait_ge(win_added[b], i * 16)
                    pool.sem_inc(passed, 1)
                    pool.tensor_copy(row_in[b][:, :],
                                     k.rows[:, bass.ds(i * 2 + b, 1)]).then_inc(win_rows[b], 1)
                    pool.wait_ge(win_rows[b], i + 1)
                    pool.sem_inc(passed, 1)
                    pool.indirect_dma_start(k.acc[layer][b],
                                            bass.IndirectOffsetOnAxis(ap=row_in[b][:, 0:1], axis=0),
                                            win_outs[b][:, :], None, compute_op=ALU.add).then_inc(win_added[b], 16)

                first = X_TILES if x_window else 0

                def stage(i, b, fetch=True, last=False):
                    if fetch:
                        before_gathers(i, b)
                    for m in range(G):
                        if fetch and m + first < G:
                            gather(i, b, m + first)
                        if not windowed and exists(i - 2):
                            scatter(i - 2, b, m)
                        if x_window and m == 4 and fetch and not last:
                            window(*((i + 1, 0) if b else (i, 1)))
                    if windowed and exists(i - 2):
                        scatter_window(i - 2, b)

                def both(i):
                    for b in (0, 1):
                        stage(i, b)

                if x_window:
                    window(0, 0)
                loop(pool, 0, LAST, both, peel=3)
                stage(LAST, 0)
                stage(LAST, 1, last=True)
                if windowed:
                    for i in (LAST - 1, LAST):
                        for b in (0, 1):
                            scatter_window(i, b)
                    for b in (0, 1):
                        pool.wait_ge(win_added[b], (LAST + 1) * 16)
                    return
                for i in (LAST + 1, LAST + 2):
                    for b in (0, 1):
                        stage(i, b, fetch=False)
                for b in (0, 1):
                    for j in range(G):
                        pool.wait_ge(added[b][j], (LAST + 1) * 16)

            choose(pool, program)

        @block.tensor
        def _(pe):
            def program(x_window, windowed):
                def fc1_of(i, b):
                    pe.wait_ge(features[b], (i + 1) * 16)
                    if due(i) or b:
                        pe.wait_ge(hid_ready[1 - b], i + b)
                    nc.tensor.matmul(hid_ps[:, 0:4 * P], fc1[:, :], ef_in[b][:, :], start=True,
                                     stop=True).then_inc(hid_psum[b], 1)

                def weights(i, b, q):
                    if q == 0:
                        pe.wait_ge(hid_ready[b], i + 1)
                    if due(i) or b or q > 1:
                        pe.wait_ge(w_ready[q % 2], nth(i, b, q))
                    half = 64 * (q // 2)
                    for j in (0, 1):
                        cols = (2 * (q % 2) + j) * P
                        ins = nc.tensor.matmul(w_ps[q % 2][0:P, j * WCOLS:(j + 1) * WCOLS],
                                               hid[b][half:half + 64, cols:cols + P], fc2[half:half + 64, :],
                                               start=True, stop=True)
                    ins.then_inc(w_psum[q % 2], 1)

                def spread_x(i, b):
                    pe.wait_ge(window_in[b], (i + 1) * 16)
                    pe.wait_ge(hot_ready, i * 2 + (b + 1))
                    if due(i) or b:
                        pe.wait_ge(x_ready, i * 2 + b)
                    for j in range(X_TILES):
                        ins = nc.tensor.matmul(x_ps[0:P, j * CH:(j + 1) * CH], hot[b][:, j * P:(j + 1) * P],
                                               xw[b][:, :], start=True, stop=True)
                    ins.then_inc(x_psum, 1)

                def turn(i, b, q):
                    if q == 0:
                        pe.wait_ge(messages[b], i + 1)
                    if due(i) or b or q:
                        pe.wait_ge(turned_ready, pair(i, b, q) * 2)
                    for j in (0, 1):
                        for c, (lo, size) in enumerate(((0, 96), (96, 128), (224, 128))):
                            ins = nc.tensor.transpose(turned_ps[j][0:size, c * P:(c + 1) * P],
                                                      msg[b][:, 2 * q + j, lo:lo + size], k.ident[0:P, 0:P])
                        ins.then_inc(turned_psum, 1)

                def map_pair(i, b, q):
                    pe.wait_ge(turned_ready, pair(i, b, q) * 2 + 2)
                    if due(i) or b or q:
                        pe.wait_ge(mapped_ready, pair(i, b, q))
                    for j in (0, 1):
                        to = mapped_ps[0:P, j * ROW:(j + 1) * ROW]
                        nc.tensor.matmul(to[:, 0:96], turned[j][0:96, 0, :], out_s[:, :], start=True, stop=True)
                        nc.tensor.matmul(to[:, 96:160], turned[j][:, 1, :], k.map_q[layer][:, :],
                                         start=True, stop=True)
                        ins = nc.tensor.matmul(to[:, 160:224], turned[j][:, 2, :], k.map_yz[layer][:, :],
                                               start=True, stop=True)
                    ins.then_inc(mapped_psum, 1)

                def sum_pair(i, b, q):
                    if q == 0:
                        pe.wait_ge(finished, i * 2 + (b + 1))
                    if due(i) or b or q:
                        pe.wait_ge(sums_ready, pair(i, b, q))
                    for j in (0, 1):
                        row = mapped[b][:, 2 * q + j, :].rearrange("p (h c) -> p h c", h=2)[:, :, 0:96]
                        ins = nc.tensor.matmul(sums_ps[0:P, j * OUT:(j + 1) * OUT], same[b][:, 2 * q + j, :],
                                               row, start=True, stop=True)
                    ins.then_inc(sums_psum, 1)

                def agg_window(i, b, j):
                    if j == 0:
                        pe.wait_ge(messages[b], i + 1)
                        pe.wait_ge(spread, i * 2 + (b + 1))
                        if due(i):
                            pe.wait_ge(win_agg[b], i)
                    ins = nc.tensor.matmul(agg_ps[b][:, 0:MSG], same_in[b][:, j, :], msg[b][:, j, :],
                                           start=j == 0, stop=j == G - 1)
                    if j == G - 1:
                        ins.then_inc(summed[b], 1)

                def transposes(i, b):
                    pe.wait_ge(win_agg[b], i + 1)
                    if due(i) or b:
                        pe.wait_ge(turned_ready, i * 2 + b)
                    for c in range(4):
                        lo = 0 if c == 0 else 96 + 128 * (c - 1)
                        ins = nc.tensor.transpose(win_T_ps[:, c * WINDOW:(c + 1) * WINDOW],
                                                  agg_sb[b][:, lo:lo + 128], k.ident[:, :])
                    ins.then_inc(turned_psum, 1)

                def map_window(i, b):
                    pe.wait_ge(turned_ready, i * 2 + (b + 1))
                    if due(i) or b:
                        pe.wait_ge(sums_ready, i * 2 + b)
                    nc.tensor.matmul(win_out_ps[:, 0:96], winT[b][0:96, 0, :], out_s[:, :],
                                     start=True, stop=True)
                    for c in range(3):
                        lo = 96 + V_CH * c
                        ins = nc.tensor.matmul(win_out_ps[:, lo:lo + V_CH], winT[b][:, 1 + c, :], out_v[:, :],
                                               start=True, stop=True)
                    ins.then_inc(sums_psum, 1)

                def windows(i, b, next_weights):
                    last = before(i, b)
                    for j in range(G):
                        agg_window(i, b, j)
                        if j % 2:
                            next_weights(j // 2)
                        if j == 2 and exists(last[0]):
                            transposes(*last)
                        if j == 5 and exists(last[0]):
                            map_window(*last)

                def pairs(i, b, next_hidden, next_weights):
                    one = before(i, b)
                    two = before(*one)
                    for q in range(4):
                        last = (i, b, q - 1) if q else (*one, 3)
                        if exists(last[0]):
                            map_pair(*last)
                        if q == 0:
                            next_hidden()
                        turn(i, b, q)
                        next_weights(q)
                        done = (*two, q + 2) if q < 2 else (*one, q - 2)
                        if exists(done[0]):
                            sum_pair(*done)

                def ahead(i, b, q):
                    weights(i, b, q)
                    if x_window and q == 1:
                        spread_x(i, b)

                for b in (0, 1):
                    fc1_of(0, b)
                    for q in range(4):
                        ahead(0, b, q)

                def slot(i, b, ahead_too=True):
                    def next_hidden():
                        if ahead_too:
                            fc1_of(i + 1, b)

                    def next_weights(q):
                        if ahead_too:
                            ahead(i + 1, b, q)

                    if windowed:
                        next_hidden()
                        windows(i, b, next_weights)
                    else:
                        pairs(i, b, next_hidden, next_weights)

                def both(i):
                    for b in (0, 1):
                        slot(i, b)

                loop(pe, 0, LAST, both, peel=2)
                for b in (0, 1):
                    slot(LAST, b, ahead_too=False)
                if windowed:
                    transposes(LAST, 1)
                    map_window(LAST, 1)
                else:
                    map_pair(LAST, 1, 3)
                    for b, q in ((0, 2), (0, 3), (1, 0), (1, 1), (1, 2), (1, 3)):
                        sum_pair(LAST, b, q)

            choose(pe, program)

        @block.scalar
        def _(act):
            def program(x_window, windowed):
                def hidden(i, b):
                    act.wait_ge(hid_psum[b], i + 1)
                    if layer == 0:
                        nc.scalar.activation(hid[b][:, :], hid_ps[:, 0:4 * P], ACT.Relu).then_inc(hid_ready[b], 1)
                    else:
                        nc.scalar.activation(hid[b][:, :], hid_ps[:, 0:4 * P], ACT.Silu,
                                             scale=HID ** -0.5).then_inc(hid_ready[b], 1)

                def weights(i, b, q):
                    if q == 0:
                        if due(i):
                            act.wait_ge(messages[b], i)
                    act.wait_ge(w_psum[q % 2], nth(i, b, q) + 1)
                    to = wts[b][:, 2 * q:2 * q + 2, :]
                    of = w_ps[q % 2][0:P, 0:2 * WCOLS].rearrange("p (j w) -> p j w", j=2)
                    if layer == 1:
                        for j in (0, 1):
                            nc.scalar.activation(to[:, j, 0:W_SV], of[:, j, 0:W_SV], ACT.Copy,
                                                 scale=e0_all[:, bass.ds((i * 2 + b) * G + (2 * q + j), 1)])
                        to, of = to[:, :, W_SV:WCOLS], of[:, :, W_SV:WCOLS]
                    nc.scalar.activation(to, of, ACT.Copy).then_inc(w_ready[q % 2], 1)

                def spread_q(i, b, tiles):
                    if 0 in tiles:
                        act.wait_ge(q_ready, i * 2 + (b + 1))
                    for j in tiles:
                        for c in range(3):
                            lo = 96 + 128 * c
                            ins = nc.scalar.activation(msg[b][:, j, lo:lo + S_CH], qs[b][:, j, :], ACT.Copy,
                                                       scale=vec_in[b][:, j, c:c + 1])
                    if G - 1 in tiles:
                        ins.then_inc(spread, 1)

                def x_out(i, b):
                    act.wait_ge(x_psum, i * 2 + (b + 1))
                    nc.scalar.activation(xg[b][:, 0:X_TILES, :].rearrange("p j c -> p (j c)"),
                                         x_ps[0:P, 0:X_TILES * CH], ACT.Copy).then_inc(x_ready, 1)

                def turned_out(i, b, q):
                    if due(i) or b or q:
                        act.wait_ge(mapped_psum, pair(i, b, q))
                    for j in (0, 1):
                        act.wait_ge(turned_psum, pair(i, b, q) * 2 + (j + 1))
                        nc.scalar.activation(turned[j][0:96, 0, :], turned_ps[j][0:96, 0:P], ACT.Copy)
                        nc.scalar.activation(turned[j][:, 1:3, :].rearrange("c m e -> c (m e)"),
                                             turned_ps[j][:, P:3 * P], ACT.Copy).then_inc(turned_ready, 1)

                def mapped_out(i, b, q):
                    if due(i):
                        act.wait_ge(sums_psum, pair(i - 1, b, q) + 1)
                    act.wait_ge(mapped_psum, pair(i, b, q) + 1)
                    nc.scalar.activation(
                        mapped[b][:, 2 * q:2 * q + 2, 0:224],
                        mapped_ps[0:P, :].rearrange("p (j c) -> p j c", j=2)[:, :, 0:224],
                        ACT.Copy).then_inc(mapped_ready, 1)

                def sums_out(i, b, q):
                    if due(i):
                        act.wait_ge(added[b][2 * q], i * 16)
                    if due(i):
                        act.wait_ge(added[b][2 * q + 1], i * 16)
                    act.wait_ge(sums_psum, pair(i, b, q) + 1)
                    nc.scalar.activation(outs[b][:, 2 * q:2 * q + 2, :].rearrange("p j c -> p (j c)"),
                                         sums_ps[0:P, 0:2 * OUT], ACT.Copy).then_inc(sums_ready, 1)

                def window_steps(i, b):
                    def window_out():
                        act.wait_ge(summed[b], i + 1)
                        nc.scalar.activation(agg_sb[b][:, :], agg_ps[b][:, 0:MSG], ACT.Copy).then_inc(win_agg[b], 1)

                    def transposed_out():
                        act.wait_ge(turned_psum, i * 2 + (b + 1))
                        nc.scalar.activation(winT[b][:, :, :].rearrange("c m e -> c (m e)"), win_T_ps[:, :],
                                             ACT.Copy).then_inc(turned_ready, 1)

                    def rows_out():
                        act.wait_ge(sums_psum, i * 2 + (b + 1))
                        if due(i):
                            act.wait_ge(win_added[b], i * 16)
                        nc.scalar.activation(win_outs[b][:, :], win_out_ps[:, 0:OUT],
                                             ACT.Copy).then_inc(sums_ready, 1)

                    return window_out, transposed_out, rows_out

                def windows(i, b, next_weights, next_spread=True):
                    last = before(i, b)
                    after = (i + 1, 0) if b else (i, 1)
                    moves = window_steps(*last) if exists(last[0]) else ()
                    for q in range(4):
                        if q in (0, 1, 3) and moves:
                            moves[(0, 1, None, 2)[q]]()
                        next_weights(q)
                        if q < 3 and next_spread:
                            spread_q(*after, range(G)[3 * q:3 * q + 3])

                def pairs(i, b, next_hidden, next_weights):
                    one = before(i, b)
                    two = before(*one)
                    for q in range(4):
                        last = (i, b, q - 1) if q else (*one, 3)
                        if exists(last[0]):
                            mapped_out(*last)
                        if q == 0:
                            next_hidden()
                        turned_out(i, b, q)
                        next_weights(q)
                        done = (*two, q + 2) if q < 2 else (*one, q - 2)
                        if exists(done[0]):
                            sums_out(*done)

                def ahead(i, b, q):
                    weights(i, b, q)
                    if x_window and q == 1:
                        x_out(i, b)

                if layer == 1:
                    act.wait_ge(e0_in, 16)
                else:
                    for n in (2, 3):
                        for m in range(ZERO_PARTS):
                            zero_part(act, k, 0, n, m)
                for b in (0, 1):
                    hidden(0, b)
                    for q in range(4):
                        ahead(0, b, q)
                if windowed:
                    spread_q(0, 0, range(G))

                def slot(i, b, ahead_too=True):
                    def next_hidden():
                        if ahead_too:
                            hidden(i + 1, b)

                    def next_weights(q):
                        if ahead_too:
                            ahead(i + 1, b, q)

                    if windowed:
                        next_hidden()
                        windows(i, b, next_weights, next_spread=ahead_too or b == 0)
                    else:
                        pairs(i, b, next_hidden, next_weights)

                def both(i):
                    for b in (0, 1):
                        slot(i, b)

                loop(act, 0, LAST, both, peel=2)
                for b in (0, 1):
                    slot(LAST, b, ahead_too=False)
                if windowed:
                    for move in window_steps(LAST, 1):
                        move()
                    return
                mapped_out(LAST, 1, 3)
                for b, q in ((0, 2), (0, 3), (1, 0), (1, 1), (1, 2), (1, 3)):
                    sums_out(LAST, b, q)

            choose(act, program)

        @block.vector
        def _(dve):
            def program(x_window, windowed):
                tt = nc.vector.tensor_tensor

                def hot_of(i, b):
                    dve.wait_ge(rows_in[b], (i + 1) * 16)
                    if due(i):
                        dve.wait_ge(x_psum, i * 2 + (b - 1))
                    nc.vector.tensor_scalar(hot[b][:, :], row_of[b][:, :],
                                            k.rows_f[:, bass.ds(i * 2 + b, 1)], None,
                                            ALU.is_equal).then_inc(hot_ready, 1)

                def products(i, b, last):
                    n = i * 2 + b

                    def reached(l):
                        dve.wait_ge(level, n * 3 + l)

                    W, X, M, e = wts[b], xg[b], msg[b], vec_in[b]
                    V = X[:, :, S_CH:CH].rearrange("p g (c m) -> p g c m", c=3)
                    if windowed:
                        MV = M[:, :, 96:MSG].rearrange("p g (c m) -> p g c m", c=3)[:, :, :, S_CH:128]
                    else:
                        MV = M[:, :, 160:FEATS].rearrange("p g (c m) -> p g c m", c=3)

                    dve.wait_ge(loaded[b], (i + 1) * 16)
                    for bank in (0, 1):
                        dve.wait_ge(w_ready[bank], nth(i, b, 2) + 1)
                    if x_window:
                        dve.wait_ge(x_ready, i * 2 + (b + 1))
                        dve.wait_ge(gathered[b], (i + 1) * (16 * (G - X_TILES)))
                    else:
                        dve.wait_ge(gathered[b], (i + 1) * (16 * G))
                    if windowed:
                        if due(i):
                            dve.wait_ge(summed[b], i)
                        dve.wait_ge(keyed[b], (i + 1) * 16)
                        nc.vector.tensor_scalar(relative[:, :], key_in[b][:, :], k.base[0:P, bass.ds(n, 1)],
                                                None, ALU.subtract)
                        tt(qs[b][:, :, :], W[:, :, W_SV:W_DOT], X[:, :, 0:S_CH], ALU.mult).then_inc(q_ready, 1)
                    else:
                        if due(i):
                            dve.wait_ge(turned_psum, i * 16 + (8 * b - 8))
                        tt(M[:, :, 96:160], W[:, :, W_SV:W_DOT], X[:, :, 0:S_CH], ALU.mult)
                    tt(d[:, :, :, :], V, bc(e[:, :, :], 3, V_CH), ALU.mult)
                    tt(y[:, :, :, :], V, bc(W[:, :, W_CROSS:WCOLS], 2, 3), ALU.mult)
                    tt(M[:, :, 0:S_CH], W[:, :, W_SS:W_VV], X[:, :, 0:S_CH], ALU.mult)
                    tt(MV[:, :, :, 0:32], V, bc(W[:, :, W_VV:W_SV], 2, 3), ALU.mult).then_inc(level, 1)
                    if x_window and not last:
                        hot_of(i + 1, b)
                    reached(1)
                    tt(cross[:, :, 2:5:2, :], bc(y[:, :, 0, :], 2, 2), bc(e[:, :, 1:3], 3, V_CH), ALU.mult)
                    tt(cross[:, :, 1:4:2, :], bc(y[:, :, 2, :], 2, 2), bc(e[:, :, 0:2], 3, V_CH), ALU.mult)
                    tt(cross[:, :, 0, :], y[:, :, 1, :], bc(e[:, :, 2], 2, V_CH), ALU.mult)
                    tt(cross[:, :, 5, :], y[:, :, 1, :], bc(e[:, :, 0], 2, V_CH), ALU.mult)
                    ins = tt(dd[:, :, :], d[:, :, 0, :], d[:, :, 1, :], ALU.add)
                    ins.then_inc(level, 1)
                    if windowed:
                        tt(same_in[b][:, :, :], bc(k.iota_row[:, :], 1, G), bc(relative[:, :], 2, WINDOW),
                           ALU.is_equal)
                    reached(2)
                    tt(dd[:, :, :], dd[:, :, :], d[:, :, 2, :], ALU.add).then_inc(level, 1)
                    tt(MV[:, :, :, 32:64], cross[:, :, 0:3, :], cross[:, :, 3:6, :], ALU.subtract)
                    reached(3)
                    tt(M[:, :, 64:96], dd[:, :, :], W[:, :, W_DOT:W_CROSS], ALU.mult).then_inc(messages[b], 1)

                def finish(i, b):
                    for j in range(G):
                        if due(i):
                            dve.wait_ge(added[b][j], i * 16)
                    dve.wait_ge(slotted, i * 2 + (b + 1))
                    nc.vector.tensor_copy(slot[b][:, :], target[:, :])
                    dve.wait_ge(mapped_ready, pair(i, b, 4))
                    part = mapped[b][:, :, 96:128]
                    vectors = mapped[b][:, :, 128:224].rearrange("p g (c m) -> p g c m", c=3)
                    tt(by_e[:, :, :, :], bc(part, 2, 3), bc(kept[b][:, :, :], 3, V_CH),
                       ALU.mult).then_inc(side_level, 1)
                    dve.wait_ge(side_level, (i * 2 + b) * 4 + 4)
                    tt(vectors, vectors, by_e[:, :, :, :], ALU.add).then_inc(finished, 1)

                def rows_to_add(i, b):
                    n = i * 2 + b

                    def reached(l):
                        dve.wait_ge(side_level, n * 4 + l)

                    S, keys_c = same[b], key_in[b][:, :]
                    dve.wait_ge(keyed[b], (i + 1) * 32)
                    if due(i):
                        dve.wait_ge(sums_psum, pair(i - 1, b, 4))
                    tt(S[:, :, :], keyrow[b][:, :, :], bc(keys_c, 2, P), ALU.is_equal).then_inc(side_level, 1)
                    reached(1)
                    for j in range(G):
                        nc.vector.tensor_tensor_reduce(
                            out=masked[:, j, :], in0=S[:, j, :], in1=k.earlier[:, :], scale=1.0,
                            scalar=0.0, op0=ALU.mult, op1=ALU.add, accum_out=count[:, j:j + 1])
                    nc.vector.tensor_scalar(away[:, :], keys_c, -1.0, k.trash[:, 0:1],
                                            ALU.mult, ALU.add).then_inc(side_level, 1)
                    reached(2)
                    nc.vector.scalar_tensor_tensor(move[:, :], count[:, :], 1.0, away[:, :],
                                                   ALU.min, ALU.mult).then_inc(side_level, 1)
                    reached(3)
                    tt(target[:, :], move[:, :], keys_c, ALU.add).then_inc(slotted, 1)

                def both(i, last=False):
                    for b in (0, 1):
                        products(i, b, last)
                        if windowed:
                            continue
                        if exists(i - 1):
                            finish(i - 1, b)
                        nc.vector.tensor_copy(kept[b][:, :, :], vec_in[b][:, :, :])
                        if exists(before(i, b)[0]):
                            rows_to_add(*before(i, b))

                if x_window:
                    hot_of(0, 0)
                    hot_of(0, 1)
                loop(dve, 0, LAST, both, peel=2)
                both(LAST, last=True)
                if not windowed:
                    finish(LAST, 0)
                    rows_to_add(LAST, 1)
                    finish(LAST, 1)

            choose(dve, program)

_WEIGHTS = {
    0: {"skip_s": "L0_gnn_W_skip0", "skip_v": "L0_gnn_W_skip1", "lin_s": "L0_gnn_W_nl0",
        "lin_v": "L0_gnn_W_nl1", "fc1": "L0_gnn_W_fc1", "fc2": "L0_gnn_W_fc2",
        "out_s": "L0_gnn_W_out_s", "out_v": "L0_gnn_W_out_v"},
    1: {"skip_s": "L1_gnn_sc_ws", "skip_v": "L1_gnn_sc_wv", "lin_s": "L1_gnn_lin1_ws",
        "lin_v": "L1_gnn_lin1_wv", "fc1": "L1_gnn_fc_w1", "fc2": "L1_gnn_fc_w2",
        "out_s": "L1_gnn_lin2_ws", "out_v": "L1_gnn_lin2_wv"},
}


def build(nc, t, out):
    ctx = ExitStack()
    with ctx:
        k = allocate(nc, ctx)
        w = {l: {name: t[full] for name, full in _WEIGHTS[l].items()} for l in (0, 1)}
        setup_phase(nc, k, w, t["ea3"], t["attr"], t["dst_col"])
        node_phase(nc, k, 0, t["x"], None)
        edge_phase(nc, k, 0, t["ef"], t["dst_col"], t["dst_row"], t["src_col"], t["src_row"], k.rhat)
        node_phase(nc, k, 1, t["x"], k.x1)
        edge_phase(nc, k, 1, t["ef"], t["src_col"], t["src_row"], t["dst_col"], t["dst_row"], t["e1"], t["e0"])
        node_phase(nc, k, 2, k.x1, out)


def kernel(**inputs):
    import concourse.bacc as bacc
    from concourse.bass_utils import run_bass_kernel_spmd

    a = {name: np.asarray(v) for name, v in inputs.items()}

    def by_component(x):
        v = x[:, S_CH:].reshape(-1, V_CH, 3).transpose(0, 2, 1).reshape(-1, 3 * V_CH)
        return np.concatenate([x[:, :S_CH], v], 1)

    def by_tile(e):
        return e.reshape(GROUPS, G, P, -1).transpose(2, 0, 1, 3)

    host = {
        "x": by_component(a["x"]).reshape(P, NT * CH),
        "ef": a["edge_attr_64"].reshape(GROUPS, 2, 4, P, HID).transpose(0, 1, 4, 2, 3).reshape(GROUPS * 128, 4 * P),
        "src_col": by_tile(a["src"]).reshape(P, -1),
        "dst_col": by_tile(a["dst"]).reshape(P, -1),
        "src_row": a["src"].reshape(GROUPS, G * P),
        "dst_row": a["dst"].reshape(GROUPS, G * P),
        "ea3": by_tile(a["edge_attr_3"]).reshape(P, -1),
        "e0": by_tile(a["edge_attr_4"][:, 0:1]).reshape(P, -1),
        "e1": by_tile(a["edge_attr_4"][:, 1:4]).reshape(P, -1),
        "attr": a["node_vec1"].reshape(P, NT),
    }
    for names in _WEIGHTS.values():
        host.update({name: a[name] for name in names.values()})
    nc = bacc.Bacc("TRN2", target_bir_lowering=False, num_devices=1)
    host = {name: np.ascontiguousarray(v) for name, v in host.items()}
    aps = {name: nc.dram_tensor(f"in_{name}", v.shape, mybir.dt.from_np(v.dtype), kind="ExternalInput").ap()
           for name, v in host.items()}
    out = nc.dram_tensor("out", [P, NT * CH], FP32, kind="ExternalOutput").ap()
    build(nc, aps, out)
    r = run_bass_kernel_spmd(nc, [{f"in_{name}": v for name, v in host.items()}], core_ids=[0])
    y = r.results[0]["out"].reshape(NODES, CH)
    v = y[:, S_CH:].reshape(NODES, 3, V_CH).transpose(0, 2, 1).reshape(NODES, 3 * V_CH)
    return np.concatenate([y[:, :S_CH], v], 1)
```
